# Optimizing a Trainium2 kernel written in Bass

```python
import numpy as np
import jax
import jax.numpy as jnp

def _softmax(x, axis=-1):
    return jax.nn.softmax(x, axis=axis)

def _gelu(x):
    return jax.nn.gelu(x, approximate=True)

def _silu(x):
    return jax.nn.silu(x)

def _sigmoid(x):
    return jax.nn.sigmoid(x)

def _layernorm(x, axis=-1, eps=1e-05):
    m = jnp.mean(x, axis=axis, keepdims=True)
    v = jnp.var(x, axis=axis, keepdims=True)
    return (x - m) / jnp.sqrt(v + eps)

def _scatter_add(tgt, idx, src, axis=0):
    return tgt.at[idx].add(src)

def _segment_sum(src, seg, n):
    return jax.ops.segment_sum(src, seg, n)
kernel_name = 'mk_cond_resid_d1_seqx_r2_6b83ad'

def setup_inputs(seed: int=0):
    np.random.seed(seed)
    _w = jnp.asarray

    def _rec_inputs():
        import jax
        import jax.numpy as jnp
        _rk = jax.random.key(seed)
        x = 7.22e-05 + 1 * jax.random.normal(jax.random.fold_in(_rk, 1), (16, 512, 512), jnp.float32)
        _lenS = 512 - jax.random.randint(jax.random.fold_in(_rk, 7), (16,), 0, max(1, 512 // 4) + 1, jnp.int32)
        _lenS2 = 512 - jax.random.randint(jax.random.fold_in(_rk, 8), (16,), 0, max(1, 512 // 4) + 1, jnp.int32)
        itok_BxS_0_999 = jax.random.randint(jax.random.fold_in(_rk, 11), (16, 512), 0, 500, jnp.int32)
        itok_BxS_0_4 = jax.random.randint(jax.random.fold_in(_rk, 12), (16, 512), 0, 5, jnp.int32)
        cond_512 = 0.00199304 + 1.00034 * jax.random.normal(jax.random.fold_in(_rk, 14), (16, 256), jnp.float32)
        cond_64 = 0.0990542 + 1.04422 * jax.random.normal(jax.random.fold_in(_rk, 15), (16, 64), jnp.float32)
        fside_Bx32_0 = -0.136436 + 0.990155 * jax.random.normal(jax.random.fold_in(_rk, 16), (16, 32), jnp.float32)
        _validS = jnp.arange(512)[None, :] < _lenS[:, None]
        _validS2 = jnp.arange(512)[None, :] < _lenS2[:, None]
        _causal = jnp.tril(jnp.ones((512, 512), dtype=bool))
        mask_BxS_ik0 = jnp.where(jnp.broadcast_to(_validS[:, :], (16, 512)), 0, 1).astype(jnp.int32)
        return (x, itok_BxS_0_999, itok_BxS_0_4, cond_512, cond_64, fside_Bx32_0, mask_BxS_ik0)
    x, itok_BxS_0_999, itok_BxS_0_4, cond_512, cond_64, fside_Bx32_0, mask_BxS_ik0 = _rec_inputs()

    def _L0_cond_setup():
        import jax, jax.numpy as jnp
        import numpy as np
        EPS = 1e-05

        def _ln(x, g, b):
            m = jnp.mean(x, axis=-1, keepdims=True)
            v = jnp.mean((x - m) ** 2, axis=-1, keepdims=True)
            return (x - m) * jax.lax.rsqrt(v + EPS) * g + b

        def _mlp_ln(s, W1, b1, W2, b2, g, b):
            h = jax.nn.silu(s @ W1 + b1) @ W2 + b2
            return _ln(h, g, b)
        key = jax.random.key(seed)
        B, S, D = (4, 1024, 512)
        MEM, NOI, RES = (256, 64, 32)
        ks = jax.random.split(key, 40)
        ki = iter(range(40))

        def nrm(shape, scale=0.02):
            return jax.random.normal(ks[next(ki)], shape, jnp.float32) * scale

        def gamma(shape):
            return jnp.ones(shape, jnp.float32) + nrm(shape)
        inp = {'x': jax.random.normal(ks[next(ki)], (B, S, D), jnp.float32), 'pathway_ids': jax.random.randint(ks[next(ki)], (B, S), 0, 500), 'compartment_ids': jax.random.randint(ks[next(ki)], (B, S), 0, 5), 'time_steps': jax.random.randint(ks[next(ki)], (B, S), 0, 5), 'scale_type': jax.random.randint(ks[next(ki)], (B, S), 0, 3), 'memory_state': jax.random.normal(ks[next(ki)], (B, MEM), jnp.float32), 'noise_state': jax.random.normal(ks[next(ki)], (B, NOI), jnp.float32), 'resource_state': jax.random.normal(ks[next(ki)], (B, RES), jnp.float32), 'pw_g': gamma((500, D)), 'pw_b': nrm((500, D)), 'cp_g': gamma((5, D)), 'cp_b': nrm((5, D)), 'tm_g': gamma((5, D)), 'tm_b': nrm((5, D)), 'ms_g': gamma((3, D)), 'ms_b': nrm((3, D)), 'mem_W1': nrm((MEM, D)), 'mem_b1': jnp.zeros((D,)), 'mem_W2': nrm((D, D)), 'mem_b2': jnp.zeros((D,)), 'mem_g': gamma((D,)), 'mem_be': jnp.zeros((D,)), 'noi_W1': nrm((NOI, D)), 'noi_b1': jnp.zeros((D,)), 'noi_W2': nrm((D, D)), 'noi_b2': jnp.zeros((D,)), 'noi_g': gamma((D,)), 'noi_be': jnp.zeros((D,)), 'res_W1': nrm((RES, D)), 'res_b1': jnp.zeros((D,)), 'res_W2': nrm((D, D)), 'res_b2': jnp.zeros((D,)), 'res_g': gamma((D,)), 'res_be': jnp.zeros((D,)), 'int_W1': nrm((6 * D, D)), 'int_b1': jnp.zeros((D,)), 'int_W2': nrm((D, D)), 'int_b2': jnp.zeros((D,)), 'int_g': gamma((D,)), 'int_be': jnp.zeros((D,)), 'aw': jnp.ones((6,), jnp.float32) / 6.0}
        return inp
    _L0_cond_all = _L0_cond_setup()
    _L0_cond_in = {k: v for k, v in _L0_cond_all.items() if k in ('pw_g', 'pw_b', 'cp_g', 'cp_b', 'tm_g', 'tm_b', 'ms_g', 'ms_b', 'mem_W1', 'mem_b1', 'mem_W2', 'mem_b2', 'mem_g', 'mem_be', 'noi_W1', 'noi_b1', 'noi_W2', 'noi_b2', 'noi_g', 'noi_be', 'res_W1', 'res_b1', 'res_W2', 'res_b2', 'res_g', 'res_be', 'int_W1', 'int_b1', 'int_W2', 'int_b2', 'int_g', 'int_be', 'aw')}
    del _L0_cond_all
    return {'x': x, 'itok_BxS_0_999': itok_BxS_0_999, 'itok_BxS_0_4': itok_BxS_0_4, 'cond_512': cond_512, 'cond_64': cond_64, 'fside_Bx32_0': fside_Bx32_0, 'mask_BxS_ik0': mask_BxS_ik0, 'L0_cond_pw_g': _L0_cond_in['pw_g'], 'L0_cond_pw_b': _L0_cond_in['pw_b'], 'L0_cond_cp_g': _L0_cond_in['cp_g'], 'L0_cond_cp_b': _L0_cond_in['cp_b'], 'L0_cond_tm_g': _L0_cond_in['tm_g'], 'L0_cond_tm_b': _L0_cond_in['tm_b'], 'L0_cond_ms_g': _L0_cond_in['ms_g'], 'L0_cond_ms_b': _L0_cond_in['ms_b'], 'L0_cond_mem_W1': _L0_cond_in['mem_W1'], 'L0_cond_mem_b1': _L0_cond_in['mem_b1'], 'L0_cond_mem_W2': _L0_cond_in['mem_W2'], 'L0_cond_mem_b2': _L0_cond_in['mem_b2'], 'L0_cond_mem_g': _L0_cond_in['mem_g'], 'L0_cond_mem_be': _L0_cond_in['mem_be'], 'L0_cond_noi_W1': _L0_cond_in['noi_W1'], 'L0_cond_noi_b1': _L0_cond_in['noi_b1'], 'L0_cond_noi_W2': _L0_cond_in['noi_W2'], 'L0_cond_noi_b2': _L0_cond_in['noi_b2'], 'L0_cond_noi_g': _L0_cond_in['noi_g'], 'L0_cond_noi_be': _L0_cond_in['noi_be'], 'L0_cond_res_W1': _L0_cond_in['res_W1'], 'L0_cond_res_b1': _L0_cond_in['res_b1'], 'L0_cond_res_W2': _L0_cond_in['res_W2'], 'L0_cond_res_b2': _L0_cond_in['res_b2'], 'L0_cond_res_g': _L0_cond_in['res_g'], 'L0_cond_res_be': _L0_cond_in['res_be'], 'L0_cond_int_W1': _L0_cond_in['int_W1'], 'L0_cond_int_b1': _L0_cond_in['int_b1'], 'L0_cond_int_W2': _L0_cond_in['int_W2'], 'L0_cond_int_b2': _L0_cond_in['int_b2'], 'L0_cond_int_g': _L0_cond_in['int_g'], 'L0_cond_int_be': _L0_cond_in['int_be'], 'L0_cond_aw': _L0_cond_in['aw']}

def reference(x, itok_BxS_0_999, itok_BxS_0_4, cond_512, cond_64, fside_Bx32_0, mask_BxS_ik0, L0_cond_pw_g, L0_cond_pw_b, L0_cond_cp_g, L0_cond_cp_b, L0_cond_tm_g, L0_cond_tm_b, L0_cond_ms_g, L0_cond_ms_b, L0_cond_mem_W1, L0_cond_mem_b1, L0_cond_mem_W2, L0_cond_mem_b2, L0_cond_mem_g, L0_cond_mem_be, L0_cond_noi_W1, L0_cond_noi_b1, L0_cond_noi_W2, L0_cond_noi_b2, L0_cond_noi_g, L0_cond_noi_be, L0_cond_res_W1, L0_cond_res_b1, L0_cond_res_W2, L0_cond_res_b2, L0_cond_res_g, L0_cond_res_be, L0_cond_int_W1, L0_cond_int_b1, L0_cond_int_W2, L0_cond_int_b2, L0_cond_int_g, L0_cond_int_be, L0_cond_aw):
    import jax
    import jax.numpy as jnp

    def _L0_cond_ref(x, pathway_ids, compartment_ids, time_steps, scale_type, memory_state, noise_state, resource_state, pw_g, pw_b, cp_g, cp_b, tm_g, tm_b, ms_g, ms_b, mem_W1, mem_b1, mem_W2, mem_b2, mem_g, mem_be, noi_W1, noi_b1, noi_W2, noi_b2, noi_g, noi_be, res_W1, res_b1, res_W2, res_b2, res_g, res_be, int_W1, int_b1, int_W2, int_b2, int_g, int_be, aw):
        import jax, jax.numpy as jnp
        import numpy as np
        EPS = 1e-05

        def _ln(x, g, b):
            m = jnp.mean(x, axis=-1, keepdims=True)
            v = jnp.mean((x - m) ** 2, axis=-1, keepdims=True)
            return (x - m) * jax.lax.rsqrt(v + EPS) * g + b

        def _mlp_ln(s, W1, b1, W2, b2, g, b):
            h = jax.nn.silu(s @ W1 + b1) @ W2 + b2
            return _ln(h, g, b)
        h = _ln(x, pw_g[pathway_ids], pw_b[pathway_ids])
        h = _ln(h, cp_g[compartment_ids], cp_b[compartment_ids])
        t = _ln(x, tm_g[time_steps], tm_b[time_steps])
        m = x + _mlp_ln(memory_state, mem_W1, mem_b1, mem_W2, mem_b2, mem_g, mem_be)[:, None, :]
        n = x + _mlp_ln(noise_state, noi_W1, noi_b1, noi_W2, noi_b2, noi_g, noi_be)[:, None, :]
        r = x + _mlp_ln(resource_state, res_W1, res_b1, res_W2, res_b2, res_g, res_be)[:, None, :]
        s = _ln(x, ms_g[scale_type], ms_b[scale_type])
        w = jax.nn.softmax(aw)
        cat = jnp.concatenate([w[0] * h, w[1] * t, w[2] * m, w[3] * n, w[4] * r, w[5] * s], axis=-1)
        return _mlp_ln(cat, int_W1, int_b1, int_W2, int_b2, int_g, int_be)
    x = x + _L0_cond_ref(x, itok_BxS_0_999, itok_BxS_0_4, itok_BxS_0_4, mask_BxS_ik0, cond_512, cond_64, fside_Bx32_0, L0_cond_pw_g, L0_cond_pw_b, L0_cond_cp_g, L0_cond_cp_b, L0_cond_tm_g, L0_cond_tm_b, L0_cond_ms_g, L0_cond_ms_b, L0_cond_mem_W1, L0_cond_mem_b1, L0_cond_mem_W2, L0_cond_mem_b2, L0_cond_mem_g, L0_cond_mem_be, L0_cond_noi_W1, L0_cond_noi_b1, L0_cond_noi_W2, L0_cond_noi_b2, L0_cond_noi_g, L0_cond_noi_be, L0_cond_res_W1, L0_cond_res_b1, L0_cond_res_W2, L0_cond_res_b2, L0_cond_res_g, L0_cond_res_be, L0_cond_int_W1, L0_cond_int_b1, L0_cond_int_W2, L0_cond_int_b2, L0_cond_int_g, L0_cond_int_be, L0_cond_aw)
    return x

_drawn_inputs = setup_inputs


def setup_inputs(seed=0):
    import zlib

    import numpy as np

    out = dict(_drawn_inputs(seed))
    spreads = {'L0_cond_mem_b1': (0.0, 0.412),
     'L0_cond_mem_b2': (0.0, 0.1),
     'L0_cond_mem_be': (0.0, 0.8),
     'L0_cond_noi_b1': (0.0, 0.314),
     'L0_cond_noi_b2': (0.0, 0.1),
     'L0_cond_noi_be': (0.0, 0.703),
     'L0_cond_res_b1': (0.0, 0.378),
     'L0_cond_res_b2': (0.0, 0.1),
     'L0_cond_res_be': (0.0, 0.708),
     'L0_cond_int_b1': (0.0, 0.1),
     'L0_cond_int_b2': (0.0, 0.1),
     'L0_cond_int_be': (0.0, 0.1),
     'L0_cond_aw': (0.1666666716337204, 0.6)}
    factors = {'L0_cond_pw_g': 8.0,
     'L0_cond_pw_b': 8.0,
     'L0_cond_cp_g': 8.0,
     'L0_cond_cp_b': 8.0,
     'L0_cond_tm_g': 8.0,
     'L0_cond_tm_b': 8.0,
     'L0_cond_ms_g': 8.0,
     'L0_cond_ms_b': 8.0,
     'L0_cond_mem_g': 8.0,
     'L0_cond_noi_g': 8.0,
     'L0_cond_res_g': 8.0,
     'L0_cond_int_g': 4.424}
    for name, (base, spread) in spreads.items():
        noise = np.random.default_rng([zlib.crc32(name.encode()), seed]).standard_normal(out[name].shape)
        drawn = base * np.exp(spread * noise) if base else spread * noise
        out[name] = jnp.asarray(drawn.astype(out[name].dtype))
    for name, factor in factors.items():
        out[name] = (out[name] * factor).astype(out[name].dtype)
    return out
```

```python
from contextlib import ExitStack

import numpy as np
import concourse.bass as bass
from concourse import mybir
from concourse.alu_op_type import AluOpType as ALU

BATCHES, TOKENS, D = 16, 512, 512
P = 128
TT = TOKENS // P
FT = D // P
KT = 4 * FT
AHEAD = 3
RING = 4
STAGE = 8
EPS = 1e-5
NETS = 3
CLS_HI, CLS_LO, SCL_HI, SCL_LO = 0, 32, 64, 96

ORDER = [("x", f) for f in range(FT)]
for _f in range(FT):
    ORDER += [("t", _f), ("s", _f)]
ORDER += [("h", f) for f in range(FT)]
MOD_BEFORE = [sum(kind != "x" for kind, _ in ORDER[:k]) for k in range(KT + 1)]
TR_BEFORE = [sum(kind != "s" for kind, _ in ORDER[:k]) for k in range(KT + 1)]
NORM_BEFORE = [sum(kind in "th" for kind, _ in ORDER[:k]) for k in range(KT + 1)]
MODS, TRS, NORMS = MOD_BEFORE[KT], TR_BEFORE[KT], NORM_BEFORE[KT]
SECOND_AT = {3: 0, 5: 1, 7: 2, 9: 3}


def build(nc, x, ids, pid, clsval, identity, condT, noiT, resT, b1T, ib1T, shift_t, scales, pw,
          W1s, W2s, b2s, gs, bes, int_W1, int_W2, int_b2, int_g, int_be, aw, out):
    f32, f32r, i32 = mybir.dt.float32, mybir.dt.float32r, mybir.dt.int32
    ACT = mybir.ActivationFunctionType
    AX = mybir.AxisListType

    x_v = x.rearrange("b (p t) d -> b p t d", t=TT)
    out_v = out.rearrange("b (p t) d -> b p t d", t=TT)

    with ExitStack() as ctx:
        def sb(name, shape, dt=f32):
            return ctx.enter_context(nc.sbuf_tensor(name, shape, dt))

        def sem(name):
            return ctx.enter_context(nc.semaphore(name))

        x_sb = sb("x_sb", [P, TT, D])
        xhat = sb("xhat", [P, TT, D])
        y_sb = sb("y_sb", [P, TT, D])
        pw_rows = sb("pw_rows", [P, TT, 2 * D])
        xbe = sb("xbe", [P, 2, TT, D])
        stage = xbe[:, :, :, :].rearrange("p a t d -> p (a t) d")
        xT = sb("xT", [P, 2, TOKENS])
        v_sb = sb("v_sb", [P, 2, TOKENS])
        cat_hi = sb("cat_hi", [P, RING, TOKENS], f32r)
        cat_lo = sb("cat_lo", [P, RING, TOKENS], f32r)
        z_sb = sb("z_sb", [P, FT, TOKENS])
        hid_hi = sb("hid_hi", [P, FT, TOKENS], f32r)
        hid_lo = sb("hid_lo", [P, FT, TOKENS], f32r)
        w1_hi = sb("w1_hi", [P, KT, D], f32r)
        w1_lo = sb("w1_lo", [P, KT, D], f32r)
        w2_hi = sb("w2_hi", [P, FT, D], f32r)
        w2_lo = sb("w2_lo", [P, FT, D], f32r)
        class_tab = sb("class_tab", [P, 3, D], f32r)
        class_bias = sb("class_bias", [P, D], f32r)
        onehot = sb("onehot", [P, TOKENS], f32r)
        ids_sb = sb("ids_sb", [P, TOKENS], i32)
        b2_rows = sb("b2_rows", [P, D], f32r)
        ones = sb("ones", [P, P], f32r)
        ident = sb("ident", [P, P])
        g_bc = sb("g_bc", [P, D])
        be_bc = sb("be_bc", [P, D])
        o_sb = sb("o_sb", [P, D])
        batch_bias = sb("batch_bias", [P, FT, BATCHES])
        pid_all = sb("pid_all", [P, BATCHES * TT], i32)
        pid_now = sb("pid_now", [P, TT], i32)
        cls_val = sb("cls_val", [P, 1])
        w_mix = sb("w_mix", [P, 8])
        w_tmp = sb("w_tmp", [P, 4])
        minus_half = sb("minus_half", [P, TT])
        eps_col = sb("eps_col", [P, TT])
        xst = sb("xst", [P, TT, 6])
        xmv = sb("xmv", [P, TT, 2])
        xve = sb("xve", [P, TT])
        xrs = sb("xrs", [P, TT])
        yst = sb("yst", [P, TT, 6])
        ymv = sb("ymv", [P, TT, 2])
        yve = sb("yve", [P, TT])
        yrs = sb("yrs", [P, TT])
        fst = sb("fst", [P, TT, 6])
        fmv = sb("fmv", [P, TT, 2])
        fve = sb("fve", [P, TT])
        frs = sb("frs", [P, TT])
        sT = sb("sT", [P, 4, BATCHES])
        b1_cols = sb("b1_cols", [P, NETS * FT])
        ib1_cols = sb("ib1_cols", [P, FT])
        shift_raw = sb("shift_raw", [P, FT * 13])
        nst = sb("nst", [P, 6])
        nmv = sb("nmv", [P, 2])
        nrs = sb("nrs", [P, 2])
        flat_y = y_sb[:, :, :].rearrange("p t d -> p (t d)")
        flat_z = z_sb[:, :, :].rearrange("p t d -> p (t d)")
        netT = flat_y[:, 0:NETS * FT * P].rearrange("p (n q) -> p n q", q=P)
        shiftT = flat_z[:, 0:MODS * P].rearrange("p (n q) -> p n q", q=P)
        net_b2, net_g, net_be, net_h, mT_flat, bb_row, b2_raw, cp_raw = [
            pw_rows[:, i // 2, (i % 2) * D:(i % 2) * D + D] for i in range(8)]
        mT = mT_flat.rearrange("p (k q) -> p k q", q=P)
        tab_raw = [xT[:, 0, :], xT[:, 1, :], cp_raw]

        hid_ps = ctx.enter_context(nc.psum_tensor("hid_ps", [P, FT, D], f32))
        t_ps = ctx.enter_context(nc.psum_tensor("t_ps", [P, TOKENS], f32))
        g_ps = ctx.enter_context(nc.psum_tensor("g_ps", [P, TOKENS], f32))
        o_ps = ctx.enter_context(nc.psum_tensor("o_ps", [P, 2, D], f32))

        small_in = sem("small_in")
        zeroed = sem("zeroed")
        net_rows_in = sem("net_rows_in")
        stage_in = [sem(f"stage_in{i}") for i in range(STAGE)]
        pe_used = sem("pe_used")
        dve_used = sem("dve_used")
        act_used = sem("act_used")
        w_hi_done = sem("w_hi_done")
        w_lo_done = sem("w_lo_done")
        mix_max = sem("mix_max")
        mix_exp = sem("mix_exp")
        mix_ready = sem("mix_ready")
        tables_ready = sem("tables_ready")
        shifts_ready = sem("shifts_ready")
        net_hidden = sem("net_hidden")
        net_silu = sem("net_silu")
        net_stats = sem("net_stats")
        net_ve = sem("net_ve")
        net_rs = sem("net_rs")
        net_rows = sem("net_rows")
        net_turned = sem("net_turned")
        mT_ready = sem("mT_ready")
        bias_copied = sem("bias_copied")
        bias_turned = sem("bias_turned")
        batch_bias_ready = sem("batch_bias_ready")
        class_bias_ready = sem("class_bias_ready")
        dve_chain = sem("dve_chain")
        half_ready = sem("half_ready")
        x_in = sem("x_in")
        ids_in = sem("ids_in")
        rows_in = [sem(f"rows_in{t}") for t in range(TT)]
        pid_ready = sem("pid_ready")
        onehot_ready = sem("onehot_ready")
        xstat = sem("xstat")
        xaggr = sem("xaggr")
        xve_done = sem("xve_done")
        xrs_done = sem("xrs_done")
        xhat_done = sem("xhat_done")
        ymul = sem("ymul")
        yadd = sem("yadd")
        ystat = sem("ystat")
        yaggr = sem("yaggr")
        yve_done = sem("yve_done")
        yrs_done = sem("yrs_done")
        yhat_done = sem("yhat_done")
        fstat = sem("fstat")
        faggr = sem("faggr")
        fve_done = sem("fve_done")
        frs_done = sem("frs_done")
        fnum = sem("fnum")
        out_ready = sem("out_ready")
        xbe_done = sem("xbe_done")
        tr_ready = sem("tr_ready")
        t_copied = sem("t_copied")
        x_hi_done = sem("x_hi_done")
        x_lo_done = sem("x_lo_done")
        picked = sem("picked")
        v_done = sem("v_done")
        m_hi_done = sem("m_hi_done")
        m_lo_done = sem("m_lo_done")
        first_done = sem("first_done")
        z_done = sem("z_done")
        hid_hi_done = sem("hid_hi_done")
        hid_lo_done = sem("hid_lo_done")
        second_done = sem("second_done")
        stored = [sem(f"stored{p}") for p in range(2)]

        def wait(eng, s, value):
            if not isinstance(value, int) or value > 0:
                eng.wait_ge(s, value)

        tiles = []
        for c in range(2):
            tiles.append((W1s[0][c * P:(c + 1) * P, :], P))
        tiles.append((W1s[1], W1s[1].shape[0]))
        tiles.append((W1s[2], W1s[2].shape[0]))
        for n in range(NETS):
            for k in range(FT):
                tiles.append((W2s[n][k * P:(k + 1) * P, :], P))
        NET_TILES = len(tiles)

        def w1_block(j, k):
            return (int_W1[j * D + k * P:j * D + (k + 1) * P, :], P)
        for k in range(FT):
            for j in (2, 3, 4):
                tiles.append(w1_block(j, k))
        X_TILES = len(tiles) - NET_TILES
        MOD0 = len(tiles)
        SOURCE = {"h": 0, "t": 1, "s": 5}
        for kind, f in ORDER:
            if kind != "x":
                tiles.append(w1_block(SOURCE[kind], f))
        PE_TILES = len(tiles)
        for k in range(FT):
            tiles.append((int_W2[k * P:(k + 1) * P, :], P))

        def stage_wait(eng, n):
            eng.wait_ge(stage_in[n % STAGE], 16 * (n // STAGE + 1))

        def released(eng, n):
            if n < PE_TILES:
                eng.wait_ge(pe_used, n + 1)
            if NET_TILES <= n < MOD0:
                eng.wait_ge(dve_used, n - NET_TILES + 1)
            if n >= MOD0:
                eng.wait_ge(act_used, n - MOD0 + 1)

        block = ctx.enter_context(nc.Block())

        small_loads = [(sT[:, 0:2, :], condT.rearrange("(c p) b -> p c b", p=P)), (sT[0:64, 2, :], noiT),
                       (sT[0:32, 3, :], resT), (b1_cols[:, :], b1T), (ib1_cols[:, :], ib1T),
                       (ident[:, :], identity), (cls_val[:, :], clsval), (pid_all[:, :], pid),
                       (w_mix[:, 0:6], aw.partition_broadcast(P)), (shift_raw[:, :], shift_t),
                       (g_bc[:, :], int_g.partition_broadcast(P)), (be_bc[:, :], int_be.partition_broadcast(P))]
        row_loads = [(b2_raw[r:r + 1, :], int_b2[None, :]) for r in (0, 32)]
        for n in range(NETS):
            for dst, src in ((net_b2, b2s[n]), (net_g, gs[n]), (net_be, bes[n])):
                row_loads.append((dst[32 * n:32 * n + BATCHES, :], src.partition_broadcast(BATCHES)))
        tm_g, ms_g, cp_g = scales
        for dst, src, bases in ((tab_raw[0], tm_g, (CLS_HI, CLS_LO)), (tab_raw[1], ms_g, (SCL_HI, SCL_LO)),
                                (tab_raw[2], cp_g, (CLS_HI, CLS_LO))):
            for base in bases:
                row_loads.append((dst[base:base + src.shape[0], :], src))

        @block.sync
        def _(sp):
            def load_x(b):
                wait(sp, tr_ready, TRS * (b - 1) + FT)
                wait(sp, xhat_done, TT * b)
                wait(sp, xbe_done, TT * b)
                sp.dma_start(x_sb[:, :, :], x_v[b]).then_inc(x_in, 16)

            def load_ids(b):
                wait(sp, onehot_ready, b)
                for half in range(2):
                    sp.dma_start(ids_sb[64 * half:64 * half + 64, :],
                                 ids[half, b].partition_broadcast(64)).then_inc(ids_in, 16)

            def store(b, par):
                sp.wait_ge(out_ready, TT * (b + 1))
                sp.dma_start(out_v[b], xbe[:, par]).then_inc(stored[par], 16)

            sp.dma_start(x_sb[:, :, :], x_v[0]).then_inc(x_in, 16)
            sp.wait_ge(zeroed, 1)
            for dst, src in small_loads:
                sp.dma_start(dst, src).then_inc(small_in, 16)
            load_ids(0)
            for n, (src, rows) in enumerate(tiles):
                if n == 4:
                    sp.wait_ge(zeroed, 5)
                    for dst, row in row_loads:
                        sp.dma_start(dst, row).then_inc(net_rows_in, 16)
                if n >= STAGE:
                    released(sp, n - STAGE)
                sp.dma_start(stage[0:rows, n % STAGE, :], src).then_inc(stage_in[n % STAGE], 16)

            def chunk(b, par, first=False, last=False):
                if not last:
                    load_x(b + 1)
                    load_ids(b + 1)
                if not first:
                    store(b - 1, 1 - par)

            chunk(0, 0, first=True)
            with sp.Fori(0, BATCHES // 2 - 1) as pair:
                b = 2 * pair + 1
                chunk(b, 1)
                chunk(b + 1, 0)
            chunk(BATCHES - 1, 1, last=True)
            store(BATCHES - 1, 1)
            for par in range(2):
                sp.wait_ge(stored[par], 16 * (BATCHES // 2))

        @block.gpsimd
        def _(pool):
            def rstd(stat_sem, count, ve, ve_sem, rs, rs_sem, mv, cols, nth):
                pool.wait_ge(stat_sem, count)
                pool.tensor_tensor(ve[:, cols], mv[:, cols, 1], eps_col[:, cols], ALU.add).then_inc(ve_sem, 1)
                pool.wait_ge(ve_sem, nth)
                pool.tensor_tensor(rs[:, cols], ve[:, cols], minus_half[:, cols], ALU.pow).then_inc(rs_sem, 1)

            def x_rstd(b):
                wait(pool, xhat_done, TT * b)
                rstd(xaggr, TT * (b + 1), xve, xve_done, xrs, xrs_done, xmv, slice(0, TT), b + 1)

            def add_be(b, par):
                wait(pool, stored[par], 8 * (b - par))
                wait(pool, x_in, 16 * (b + 1))
                for t in range(TT):
                    pool.tensor_tensor(xbe[:, par, t, :], x_sb[:, t, :], be_bc[:, :], ALU.add).then_inc(xbe_done, 1)

            def pid_copy(b):
                for t in range(TT):
                    wait(pool, rows_in[t], 16 * b)
                pool.tensor_copy(pid_now[:, :], pid_all[:, bass.ds(b * TT, TT)]).then_inc(pid_ready, 1)
                pool.wait_ge(pid_ready, b + 1)

            def gather(b, t):
                wait(pool, yadd, TT * (b - 1) + t + 1)
                pool.nop(nofuse=True)
                pool.indirect_dma_start(pw_rows[:, t, :], None, pw[:, :],
                                        bass.IndirectOffsetOnAxis(ap=pid_now[:, t:t + 1], axis=0)
                                        ).then_inc(rows_in[t], 16)

            def low_part(b, kk):
                n = MODS * b + MOD_BEFORE[kk]
                if ORDER[kk][0] == "x":
                    return
                pool.wait_ge(m_hi_done, n + 1)
                pool.tensor_tensor(cat_lo[:, kk % RING, :], v_sb[:, MOD_BEFORE[kk] % 2, :],
                                   cat_hi[:, kk % RING, :].bitcast(f32), ALU.subtract).then_inc(m_lo_done, 1)

            def hidden_low(b, h):
                pool.wait_ge(hid_hi_done, FT * b + h + 1)
                pool.tensor_tensor(hid_lo[:, h, :], z_sb[:, h, :], hid_hi[:, h, :].bitcast(f32),
                                   ALU.subtract).then_inc(hid_lo_done, 1)

            pool.memset(sT[:, :, :], 0.0).then_inc(zeroed, 1)
            pool.memset(pw_rows[:, :, :], 0.0).then_inc(zeroed, 1)
            pool.memset(xT[:, :, :], 0.0).then_inc(zeroed, 1)
            pool.memset(netT, 0.0).then_inc(zeroed, 1)
            pool.memset(shiftT, 0.0).then_inc(zeroed, 1)
            pool.memset(minus_half[:, :], -0.5).then_inc(half_ready, 1)
            pool.memset(nrs[:, :], 0.0).then_inc(hid_lo_done, FT)
            pool.memset(eps_col[:, :], EPS).then_inc(half_ready, 1)
            pool.wait_ge(half_ready, 2)
            x_rstd(0)
            pool.wait_ge(net_stats, 1)
            pool.tensor_scalar(nrs[:, 0:1], nmv[:, 1:2], EPS, None, ALU.add).then_inc(net_ve, 1)
            pool.wait_ge(net_ve, 1)
            pool.tensor_tensor(nrs[:, 1:2], nrs[:, 0:1], minus_half[:, 0:1], ALU.pow).then_inc(net_rs, 1)
            pool.wait_ge(small_in, 16 * len(small_loads))
            pool.wait_ge(batch_bias_ready, FT)
            pool.wait_ge(tables_ready, 1)
            pid_copy(0)
            for t in range(TT):
                gather(0, t)
            pool.wait_ge(act_used, len(tiles) - MOD0)
            pool.wait_ge(pe_used, PE_TILES)
            add_be(0, 0)

            def chunk(b, par, first=False, last=False):
                for k in range(KT):
                    kk = k + AHEAD
                    if kk < KT:
                        low_part(b, kk)
                    elif not last:
                        low_part(b + 1, kk - KT)
                    if not first and k < 2:
                        hidden_low(b - 1, 2 * k)
                        hidden_low(b - 1, 2 * k + 1)
                    if k % 2 == 1 and k < 8:
                        t = k // 2
                        rstd(yaggr, TT * b + t + 1, yve, yve_done, yrs, yrs_done, ymv, slice(t, t + 1), TT * b + t + 1)
                    if not first and k in (4, 6, 8, 10):
                        t = (k - 4) // 2
                        rstd(faggr, TT * (b - 1) + t + 1, fve, fve_done, frs, frs_done, fmv, slice(t, t + 1),
                             TT * (b - 1) + t + 1)
                    if not last:
                        if k == 8:
                            pid_copy(b + 1)
                        if k in (8, 9, 10, 11):
                            gather(b + 1, k - 8)
                        if k == 12:
                            x_rstd(b + 1)
                        if k == 14:
                            add_be(b + 1, 1 - par)

            chunk(0, 0, first=True)
            with pool.Fori(0, BATCHES // 2 - 1) as pair:
                b = 2 * pair + 1
                chunk(b, 1)
                chunk(b + 1, 0)
            chunk(BATCHES - 1, 1, last=True)
            hidden_tail = BATCHES - 1
            for h in range(FT):
                hidden_low(hidden_tail, h)
            for t in range(TT):
                rstd(faggr, TT * hidden_tail + t + 1, fve, fve_done, frs, frs_done, fmv, slice(t, t + 1),
                     TT * hidden_tail + t + 1)

        @block.scalar
        def _(act):
            act.wait_ge(mix_max, 1)
            act.activation(w_mix[:, 0:6], w_mix[:, 0:6], ACT.Exp, bias=w_tmp[:, 0:1]).then_inc(mix_exp, 1)
            act.wait_ge(net_hidden, 1)
            act.wait_ge(zeroed, 5)
            act.wait_ge(small_in, 16 * len(small_loads))
            for n in range(NETS):
                for k in range(FT):
                    i = n * FT + k
                    act.activation(netT[:, i, 32 * n:32 * n + BATCHES], o_ps[:, 0, i * BATCHES:(i + 1) * BATCHES],
                                   ACT.Silu, bias=b1_cols[:, i:i + 1]).then_inc(net_silu, 1)
            act.wait_ge(mix_ready, 1)
            for k in range(FT):
                act.wait_ge(dve_used, NETS * (k + 1))
                act.activation(w1_hi[:, k, :], v_sb[:, k % 2, :], ACT.Copy).then_inc(w_hi_done, 1)
            for n in range(MOD0, len(tiles)):
                i = FT + n - MOD0
                stage_wait(act, n)
                act.wait_ge(w_lo_done, i - 1)
                if n < PE_TILES:
                    j = SOURCE[ORDER[i][0]]
                    act.activation(v_sb[:, i % 2, :], stage[:, n % STAGE, :], ACT.Copy,
                                   scale=w_mix[:, j:j + 1]).then_inc(act_used, 1)
                    dst = w1_hi[:, i, :]
                else:
                    act.activation(v_sb[:, i % 2, :], stage[:, n % STAGE, :], ACT.Copy).then_inc(act_used, 1)
                    dst = w2_hi[:, n - PE_TILES, :]
                act.wait_ge(act_used, n - MOD0 + 1)
                act.activation(dst, v_sb[:, i % 2, :], ACT.Copy).then_inc(w_hi_done, 1)
            act.wait_ge(w_lo_done, KT + FT)
            act.wait_ge(tables_ready, 1)
            act.wait_ge(batch_bias_ready, FT)

            def make(b, kk):
                kind, f = ORDER[kk]
                if kind == "x":
                    act.wait_ge(tr_ready, TRS * b + TR_BEFORE[kk] + 1)
                    wait(act, first_done, FT * (KT * b + kk - RING + 1))
                    act.activation(cat_hi[:, kk % RING, :], t_ps[:, :], ACT.Copy).then_inc(x_hi_done, 1)
                    return
                if kind in "th":
                    act.wait_ge(tr_ready, TRS * b + TR_BEFORE[kk] + 1)
                    wait(act, v_done, MODS * b + MOD_BEFORE[kk] - (1 if (kind == "h") == (f > 0) and not (kind == "t" and f > 0) else 2))
                    act.activation(xT[:, NORM_BEFORE[kk] % 2, :], t_ps[:, :], ACT.Copy).then_inc(t_copied, 1)
                act.wait_ge(v_done, MODS * b + MOD_BEFORE[kk] + 1)
                wait(act, first_done, FT * (KT * b + kk - RING + 1))
                act.activation(cat_hi[:, kk % RING, :], v_sb[:, MOD_BEFORE[kk] % 2, :], ACT.Copy).then_inc(m_hi_done, 1)

            def hidden(b, h):
                act.wait_ge(first_done, FT * (KT * b + KT - 1) + h + 1)
                act.wait_ge(hid_lo_done, FT * b + h + 1)
                act.activation(z_sb[:, h, :], hid_ps[:, h, :], ACT.Silu,
                               bias=batch_bias[:, h, bass.ds(b, 1)]).then_inc(z_done, 1)

            def hidden_high(b, h):
                act.wait_ge(z_done, FT * b + h + 1)
                act.wait_ge(second_done, TT * (b + 1))
                act.activation(hid_hi[:, h, :], z_sb[:, h, :], ACT.Copy).then_inc(hid_hi_done, 1)

            for kk in range(AHEAD):
                make(0, kk)

            def chunk(b, first=False, last=False):
                for k in range(KT):
                    if not first and k == 0:
                        for h in range(FT):
                            hidden(b - 1, h)
                    kk = k + AHEAD
                    if kk < KT:
                        make(b, kk)
                    elif not last:
                        make(b + 1, kk - KT)
                    if not first and k < 2:
                        hidden_high(b - 1, 2 * k)
                        hidden_high(b - 1, 2 * k + 1)

            chunk(0, first=True)
            with act.Fori(0, BATCHES // 2 - 1) as pair:
                b = 2 * pair + 1
                chunk(b)
                chunk(b + 1)
            chunk(BATCHES - 1, last=True)
            for h in range(FT):
                hidden(BATCHES - 1, h)
            for h in range(FT):
                hidden_high(BATCHES - 1, h)

        @block.vector
        def _(dve):
            def x_stats(b, t):
                if t == 0:
                    dve.wait_ge(x_in, 16 * (b + 1))
                dve.bn_stats(xst[:, t, :], x_sb[:, t, :]).then_inc(xstat, 1)
                dve.wait_ge(xstat, TT * b + t + 1)
                dve.nop(nofuse=True)
                dve.bn_aggr(xmv[:, t, :], xst[:, t, :]).then_inc(xaggr, 1)

            def x_norm(b, t):
                dve.wait_ge(xrs_done, b + 1)
                if t == 0:
                    wait(dve, tr_ready, TRS * (b - 1) + TR_BEFORE[KT - FT])
                    wait(dve, ymul, TT * b)
                dve.tensor_scalar(xhat[:, t, :], x_sb[:, t, :], xmv[:, t, 0:1], xrs[:, t:t + 1],
                                  ALU.subtract, ALU.mult).then_inc(xhat_done, 1)

            def y_mul(b, t):
                dve.wait_ge(rows_in[t], 16 * (b + 1))
                dve.wait_ge(xhat_done, TT * (b + 1))
                wait(dve, tr_ready, TRS * b)
                dve.tensor_tensor(y_sb[:, t, :], xhat[:, t, :], pw_rows[:, t, 0:D], ALU.mult).then_inc(ymul, 1)

            def y_add(b, t):
                n = TT * b + t + 1
                dve.wait_ge(ymul, n)
                dve.tensor_tensor(y_sb[:, t, :], y_sb[:, t, :], pw_rows[:, t, D:2 * D], ALU.add).then_inc(yadd, 1)
                dve.wait_ge(yadd, n)
                dve.bn_stats(yst[:, t, :], y_sb[:, t, :]).then_inc(ystat, 1)
                dve.wait_ge(ystat, n)
                dve.nop(nofuse=True)
                dve.bn_aggr(ymv[:, t, :], yst[:, t, :]).then_inc(yaggr, 1)

            def y_norm(b, t):
                dve.wait_ge(yrs_done, TT * b + t + 1)
                dve.tensor_scalar(y_sb[:, t, :], y_sb[:, t, :], ymv[:, t, 0:1], yrs[:, t:t + 1],
                                  ALU.subtract, ALU.mult).then_inc(yhat_done, 1)

            def compare(b):
                dve.wait_ge(ids_in, 32 * (b + 1))
                wait(dve, picked, MODS * b)
                dve.tensor_scalar(onehot[:, :], ids_sb[:, :], cls_val[:, 0:1], None, ALU.is_equal).then_inc(onehot_ready, 1)

            def make(b, kk):
                kind, f = ORDER[kk]
                if kind == "x":
                    dve.wait_ge(x_hi_done, FT * b + f + 1)
                    dve.tensor_tensor(cat_lo[:, kk % RING, :], t_ps[:, :], cat_hi[:, kk % RING, :].bitcast(f32),
                                      ALU.subtract).then_inc(x_lo_done, 1)
                    return
                n = MODS * b + MOD_BEFORE[kk]
                dve.wait_ge(t_copied, NORMS * b + NORM_BEFORE[kk] + (kind != "s"))
                dve.wait_ge(picked, n + 1)
                wait(dve, m_lo_done, n - 1)
                slot = (NORM_BEFORE[kk] - (kind == "s")) % 2
                dve.tensor_tensor(v_sb[:, MOD_BEFORE[kk] % 2, :], g_ps[:, :], xT[:, slot, :], ALU.mult).then_inc(v_done, 1)

            def out_stats(b, t):
                n = TT * b + t + 1
                dve.wait_ge(second_done, n + TT)
                dve.bn_stats(fst[:, t, :], o_ps[:, t % 2, :]).then_inc(fstat, 1)
                dve.wait_ge(fstat, n)
                dve.nop(nofuse=True)
                dve.bn_aggr(fmv[:, t, :], fst[:, t, :]).then_inc(faggr, 1)
                dve.wait_ge(faggr, n)
                wait(dve, out_ready, n - 1)
                dve.scalar_tensor_tensor(o_sb[:, :], o_ps[:, t % 2, :], fmv[:, t, 0:1], g_bc[:, :],
                                         ALU.subtract, ALU.mult).then_inc(fnum, 1)

            def out_sum(b, t, par):
                n = TT * b + t + 1
                dve.wait_ge(fnum, n + 1)
                dve.wait_ge(frs_done, n)
                dve.wait_ge(xbe_done, n)
                dve.scalar_tensor_tensor(xbe[:, par, t, :], o_sb[:, :], frs[:, t:t + 1], xbe[:, par, t, :],
                                         ALU.mult, ALU.add).then_inc(out_ready, 1)

            def link(ins):
                links[0] += 1
                ins.then_inc(dve_chain, 1)
                dve.wait_ge(dve_chain, links[0])

            links = [0]
            for t in range(TT):
                x_stats(0, t)
            dve.wait_ge(small_in, 16 * len(small_loads))
            link(dve.reduce_max(w_tmp[:, 1:2], w_mix[:, 0:6], AX.X))
            dve.tensor_scalar(w_tmp[:, 0:1], w_tmp[:, 1:2], -1.0, None, ALU.mult).then_inc(mix_max, 1)
            dve.wait_ge(mix_exp, 1)
            link(dve.reduce_sum(w_tmp[:, 2:3], w_mix[:, 0:6], AX.X))
            link(dve.reciprocal(w_tmp[:, 3:4], w_tmp[:, 2:3]))
            dve.tensor_scalar(w_mix[:, 0:6], w_mix[:, 0:6], w_tmp[:, 3:4], None, ALU.mult).then_inc(mix_ready, 1)
            dve.wait_ge(mix_ready, 1)
            dve.wait_ge(zeroed, 5)
            raw_at = 0
            for j, at, step, n_cls, bases in ((1, 0, 2, 5, (CLS_HI, CLS_LO)), (5, 1, 2, 3, (SCL_HI, SCL_LO)),
                                              (0, 2 * FT, 1, 5, (CLS_HI, CLS_LO))):
                src = shift_raw[:, raw_at:raw_at + FT * n_cls].rearrange("p (k c) -> p k c", c=n_cls)
                for base in bases:
                    dve.tensor_scalar(shiftT[:, at:at + (FT - 1) * step + 1:step, base:base + n_cls], src,
                                      w_mix[:, j:j + 1], None, ALU.mult).then_inc(shifts_ready, 1)
                raw_at += FT * n_cls
            dve.memset(ones[:, :].bitcast(f32), 1.0).then_inc(fnum, 1)
            dve.wait_ge(net_rows_in, 16 * len(row_loads))
            for i in range(3):
                link(dve.tensor_copy(class_tab[:, i, :], tab_raw[i]))
            link(dve.tensor_copy(b2_rows[:, :], b2_raw))
            for i, base in enumerate((CLS_LO, SCL_LO, CLS_LO)):
                rows = slice(base, base + 32)
                link(dve.tensor_tensor(class_tab[rows, i, :], tab_raw[i][rows],
                                       class_tab[rows, i, :].bitcast(f32), ALU.subtract))
            dve.tensor_tensor(b2_rows[32:64, :], b2_raw[32:64], b2_rows[32:64, :].bitcast(f32),
                              ALU.subtract).then_inc(tables_ready, 1)
            compare(0)
            for t in range(TT):
                x_norm(0, t)
            dve.wait_ge(pe_used, NET_TILES)
            link(dve.tensor_tensor(net_h, o_ps[:, 1, :], net_b2, ALU.add))
            link(dve.bn_stats(nst[:, :], net_h))
            dve.bn_aggr(nmv[:, :], nst[:, :]).then_inc(net_stats, 1)
            dve.wait_ge(net_rs, 1)
            link(dve.tensor_scalar(net_h, net_h, nmv[:, 0:1], nrs[:, 1:2], ALU.subtract, ALU.mult))
            link(dve.tensor_tensor(net_h, net_h, net_g, ALU.mult))
            dve.tensor_tensor(net_h, net_h, net_be, ALU.add).then_inc(net_rows, 1)
            dve.wait_ge(net_turned, 1)
            turned = t_ps[:, :].rearrange("p (k q) -> p k q", q=P)
            for n in range(NETS):
                cols = slice(32 * n, 32 * n + BATCHES)
                dve.tensor_scalar(mT[:, :, cols], turned[:, :, cols], w_mix[:, 2 + n:3 + n], None,
                                  ALU.mult).then_inc(mT_ready, 1)

            def weight_low(i, dst_hi, dst_lo):
                dve.wait_ge(w_hi_done, i + 1)
                dve.tensor_tensor(dst_lo, v_sb[:, i % 2, :], dst_hi.bitcast(f32), ALU.subtract).then_inc(w_lo_done, 1)

            for k in range(FT):
                n = NET_TILES + NETS * k
                v = v_sb[:, k % 2, :]
                for j in range(NETS):
                    stage_wait(dve, n + j)
                    raw = stage[:, (n + j) % STAGE, :]
                    if j == 0:
                        ins = dve.tensor_scalar(v, raw, w_mix[:, 2:3], None, ALU.mult)
                    else:
                        ins = dve.scalar_tensor_tensor(v, raw, w_mix[:, 2 + j:3 + j], v, ALU.mult, ALU.add)
                    ins.then_inc(dve_used, 1)
                    dve.wait_ge(dve_used, NETS * k + j + 1)
                weight_low(k, w1_hi[:, k, :], w1_lo[:, k, :])
            dve.wait_ge(pe_used, MOD0)
            dve.tensor_copy(bb_row[0:BATCHES, :], hid_ps[0:BATCHES, 0, :]).then_inc(bias_copied, 1)
            dve.wait_ge(bias_turned, 1)
            for h in range(FT):
                dve.tensor_scalar(batch_bias[:, h, :], t_ps[:, h * BATCHES:(h + 1) * BATCHES], ib1_cols[:, h:h + 1],
                                  None, ALU.add).then_inc(batch_bias_ready, 1)
            for i in range(FT, KT):
                weight_low(i, w1_hi[:, i, :], w1_lo[:, i, :])
            for k in range(FT):
                weight_low(KT + k, w2_hi[:, k, :], w2_lo[:, k, :])
            dve.wait_ge(pe_used, PE_TILES)
            link(dve.tensor_copy(class_bias[:, :], hid_ps[:, 1, :]))
            for base in (CLS_LO, SCL_LO):
                rows = slice(base, base + 32)
                dve.tensor_tensor(class_bias[rows, :], hid_ps[rows, 1, :], class_bias[rows, :].bitcast(f32),
                                  ALU.subtract).then_inc(class_bias_ready, 1)
            for kk in range(AHEAD):
                make(0, kk)

            def chunk(b, par, first=False, last=False):
                for k in range(KT):
                    kk = k + AHEAD
                    if kk < KT:
                        make(b, kk)
                    elif not last:
                        make(b + 1, kk - KT)
                    if k % 2 == 0 and 2 <= k <= 8:
                        y_norm(b, k // 2 - 1)
                    if k < 8:
                        (y_add if k % 2 else y_mul)(b, k // 2)
                    if not first and k in (4, 6, 8, 10):
                        out_stats(b - 1, (k - 4) // 2)
                    if not first and k in (5, 7, 9, 11):
                        out_sum(b - 1, (k - 5) // 2, 1 - par)
                    if not last:
                        if k in (8, 9, 10, 11):
                            x_stats(b + 1, k - 8)
                        if k == 13:
                            compare(b + 1)
                        if k in (14, 15):
                            x_norm(b + 1, 2 * (k - 14))
                            x_norm(b + 1, 2 * (k - 14) + 1)

            chunk(0, 0, first=True)
            with dve.Fori(0, BATCHES // 2 - 1) as pair:
                b = 2 * pair + 1
                chunk(b, 1)
                chunk(b + 1, 0)
            chunk(BATCHES - 1, 1, last=True)
            for t in range(TT):
                out_stats(BATCHES - 1, t)
                out_sum(BATCHES - 1, t, 1)

        @block.tensor
        def _(pe):
            pe.wait_ge(small_in, 16 * len(small_loads))
            for n in range(4):
                stage_wait(pe, n)
            pe.transpose(t_ps[:, 0:P], ident[:, :], ident[:, :]).then_inc(second_done, TT)
            for n in range(NETS):
                parts = ((0, P, 0), (1, P, 1)) if n == 0 else ((n + 1, tiles[n + 1][1], n + 1),)
                for h in range(FT):
                    i = n * FT + h
                    for tile, rows, col in parts:
                        ins = pe.matmul(o_ps[:, 0, i * BATCHES:(i + 1) * BATCHES],
                                        stage[0:rows, tile, h * P:(h + 1) * P], sT[0:rows, col, :],
                                        start=(tile == parts[0][0]), stop=(tile == parts[-1][0]))
            ins.then_inc(net_hidden, 1)
            pe.wait_ge(net_silu, NETS * FT)
            for i in range(NETS * FT):
                stage_wait(pe, 4 + i)
                ins = pe.matmul(o_ps[:, 1, :], netT[:, i, :], stage[:, (4 + i) % STAGE, :],
                                start=(i == 0), stop=(i == NETS * FT - 1))
                ins.then_inc(pe_used, 5 if i == 0 else 1)
            pe.wait_ge(pe_used, NET_TILES)
            pe.wait_ge(net_rows, 1)
            for k in range(FT):
                ins = pe.transpose(t_ps[:, k * P:(k + 1) * P], net_h[:, k * P:(k + 1) * P], ident[:, :])
            ins.then_inc(net_turned, 1)
            pe.wait_ge(mT_ready, NETS)
            for k in range(FT):
                for j in range(NETS):
                    n = NET_TILES + NETS * k + j
                    stage_wait(pe, n)
                    ins = pe.matmul(hid_ps[0:BATCHES, 0, :], mT[:, k, 32 * j:32 * j + BATCHES],
                                    stage[:, n % STAGE, :], start=(k + j == 0), stop=(n == MOD0 - 1))
                    ins.then_inc(pe_used, 1)
            pe.wait_ge(bias_copied, 1)
            for h in range(FT):
                ins = pe.transpose(t_ps[:, h * BATCHES:(h + 1) * BATCHES], bb_row[0:BATCHES, h * P:(h + 1) * P],
                                   ident[0:BATCHES, 0:BATCHES])
            ins.then_inc(bias_turned, 1)
            pe.wait_ge(shifts_ready, 6)
            for n in range(MOD0, PE_TILES):
                stage_wait(pe, n)
                ins = pe.matmul(hid_ps[:, 1, :], shiftT[:, n - MOD0, :], stage[:, n % STAGE, :],
                                start=(n == MOD0), stop=(n == PE_TILES - 1))
                ins.then_inc(pe_used, 1)

            def make(b, kk):
                kind, f = ORDER[kk]
                if kind != "s":
                    if kind == "x" and f > 0:
                        pe.wait_ge(x_lo_done, FT * b + f)
                    elif kind == "t" and f == 0:
                        pe.wait_ge(x_lo_done, FT * (b + 1))
                    else:
                        wait(pe, t_copied, NORMS * b + NORM_BEFORE[kk])
                    if kind == "x":
                        pe.wait_ge(x_in, 16 * (b + 1))
                    elif f == 0:
                        pe.wait_ge(xhat_done if kind == "t" else yhat_done, TT * (b + 1))
                    src = {"x": x_sb, "t": xhat, "h": y_sb}[kind]
                    for t in range(TT):
                        ins = pe.transpose(t_ps[:, t * P:(t + 1) * P], src[:, t, f * P:(f + 1) * P], ident[:, :])
                    ins.then_inc(tr_ready, 1)
                if kind != "x":
                    wait(pe, v_done, MODS * b + MOD_BEFORE[kk])
                    pe.wait_ge(onehot_ready, b + 1)
                    pe.matmul(g_ps[:, :], class_tab[:, "tsh".index(kind), f * P:(f + 1) * P], onehot[:, :],
                              start=True, stop=True).then_inc(picked, 1)

            def first(b, k):
                if k < FT:
                    pe.wait_ge(x_lo_done, FT * b + k + 1)
                else:
                    pe.wait_ge(m_lo_done, MODS * b + MOD_BEFORE[k] + 1)
                hi, lo = cat_hi[:, k % RING, :], cat_lo[:, k % RING, :]
                for h in range(FT):
                    cols = slice(h * P, (h + 1) * P)
                    acc = hid_ps[:, h, :]
                    if k == 0:
                        wait(pe, z_done, FT * (b - 1) + h + 1)
                        pe.wait_ge(onehot_ready, b + 1)
                        pe.matmul(acc, class_bias[:, cols], onehot[:, :], start=True, stop=False)
                    pe.matmul(acc, w1_hi[:, k, cols], hi, start=False, stop=False)
                    pe.matmul(acc, w1_hi[:, k, cols], lo, start=False, stop=False)
                    pe.matmul(acc, w1_lo[:, k, cols], hi, start=False, stop=(k == KT - 1)).then_inc(first_done, 1)

            def second(b, t):
                pe.wait_ge(hid_lo_done, FT * (b + 2))
                pe.wait_ge(fnum, TT * b + t)
                cols = slice(t * P, (t + 1) * P)
                acc = o_ps[:, t % 2, :]
                pe.matmul(acc, ones[:, :], b2_rows[:, :], start=True, stop=False)
                for k in range(FT):
                    pe.matmul(acc, hid_hi[:, k, cols], w2_hi[:, k, :], start=False, stop=False)
                    pe.matmul(acc, hid_lo[:, k, cols], w2_hi[:, k, :], start=False, stop=False)
                    ins = pe.matmul(acc, hid_hi[:, k, cols], w2_lo[:, k, :], start=False, stop=(k == FT - 1))
                ins.then_inc(second_done, 1)

            pe.wait_ge(batch_bias_ready, FT)
            pe.wait_ge(tables_ready, 1)
            for kk in range(AHEAD):
                make(0, kk)
            pe.wait_ge(class_bias_ready, 2)
            pe.wait_ge(w_lo_done, KT + FT)

            def chunk(b, first_chunk=False, last=False):
                for k in range(KT):
                    kk = k + AHEAD
                    if kk < KT:
                        make(b, kk)
                    elif not last:
                        make(b + 1, kk - KT)
                    first(b, k)
                    if not first_chunk and k in SECOND_AT:
                        second(b - 1, SECOND_AT[k])

            chunk(0, first_chunk=True)
            with pe.Fori(0, BATCHES // 2 - 1) as pair:
                b = 2 * pair + 1
                chunk(b)
                chunk(b + 1)
            chunk(BATCHES - 1, last=True)
            for t in range(TT):
                second(BATCHES - 1, t)


_NETS = ["mem", "noi", "res"]


def kernel(**inputs):
    import concourse.bacc as bacc
    from concourse.bass_utils import run_bass_kernel_spmd

    nc = bacc.Bacc("TRN2", target_bir_lowering=False, num_devices=1)
    arrays = {}

    def put(name, a):
        a = np.ascontiguousarray(a)
        arrays[name] = a
        return nc.dram_tensor(name, a.shape, mybir.dt.from_np(a.dtype), kind="ExternalInput").ap()

    def given(name):
        return np.asarray(inputs[name])

    def cond(name):
        return given("L0_cond_" + name)

    def by_column(ids):
        return ids.reshape(BATCHES, P, TT).transpose(0, 2, 1).reshape(BATCHES, TOKENS)

    def cols(v):
        return v.reshape(FT, P).T

    def turned(tab):
        return tab.T.reshape(FT, P, -1).transpose(1, 0, 2).reshape(P, -1)

    cls, scl = given("itok_BxS_0_4"), given("mask_BxS_ik0")
    pathway = given("itok_BxS_0_999")
    class_of = np.full((P, 1), -1.0, np.float32)
    for base, n in ((CLS_HI, 5), (CLS_LO, 5), (SCL_HI, 3), (SCL_LO, 3)):
        class_of[base:base + n, 0] = np.arange(n)
    args = dict(
        x=put("x", given("x")),
        ids=put("ids", np.stack([by_column(cls), by_column(scl)])),
        pid=put("pid", pathway.reshape(BATCHES, P, TT).transpose(1, 0, 2).reshape(P, BATCHES * TT)),
        clsval=put("class_of", class_of),
        identity=put("identity", np.eye(P, dtype=np.float32)),
        condT=put("condT", given("cond_512").T),
        noiT=put("noiT", given("cond_64").T),
        resT=put("resT", given("fside_Bx32_0").T),
        b1T=put("b1T", np.concatenate([cols(cond(n + "_b1")) for n in _NETS], axis=1)),
        ib1T=put("ib1T", cols(cond("int_b1"))),
        shift_t=put("shift_t", np.concatenate([turned(cond(n)) for n in ("tm_b", "ms_b", "cp_b")], axis=1)),
        scales=[put(n, cond(n)) for n in ("tm_g", "ms_g", "cp_g")],
        pw=put("pw", np.concatenate([cond("pw_g"), cond("pw_b")], axis=1)),
        W1s=[put(n + "_W1", cond(n + "_W1")) for n in _NETS],
        W2s=[put(n + "_W2", cond(n + "_W2")) for n in _NETS],
        b2s=[put(n + "_b2", cond(n + "_b2")) for n in _NETS],
        gs=[put(n + "_g", cond(n + "_g")) for n in _NETS],
        bes=[put(n + "_be", cond(n + "_be")) for n in _NETS],
        int_W1=put("int_W1", cond("int_W1")), int_W2=put("int_W2", cond("int_W2")),
        int_b2=put("int_b2", cond("int_b2")), int_g=put("int_g", cond("int_g")),
        int_be=put("int_be", cond("int_be")), aw=put("aw", cond("aw")),
        out=nc.dram_tensor("out", (BATCHES, TOKENS, D), mybir.dt.float32, kind="ExternalOutput").ap(),
    )
    build(nc, **args)
    r = run_bass_kernel_spmd(nc, [arrays], core_ids=[0])
    return r.results[0]["out"]
```

```python
from contextlib import ExitStack

import numpy as np
import concourse.bass as bass
from concourse import mybir
from concourse.alu_op_type import AluOpType as ALU

BATCHES, TOKENS, D = 16, 512, 512
P = 128
TT = TOKENS // P
FT = D // P
KT = 4 * FT
AHEAD = 3
RING = 4
STAGE = 6
EPS = 1e-5
NETS = 3
CLS_HI, CLS_LO, SCL_HI, SCL_LO = 0, 32, 64, 96

ORDER = [("x", f) for f in range(FT)]
for _f in range(FT):
    ORDER += [("t", _f), ("s", _f)]
ORDER += [("h", f) for f in range(FT)]
MOD_BEFORE = [sum(kind != "x" for kind, _ in ORDER[:k]) for k in range(KT + 1)]
TR_BEFORE = [sum(kind != "s" for kind, _ in ORDER[:k]) for k in range(KT + 1)]
NORM_BEFORE = [sum(kind in "th" for kind, _ in ORDER[:k]) for k in range(KT + 1)]
MODS, TRS, NORMS = MOD_BEFORE[KT], TR_BEFORE[KT], NORM_BEFORE[KT]
SECOND_AT = {3: 0, 5: 1, 7: 2, 9: 3}
LAST_DONE = [FT * (KT - RING) + n for n in (2 * RING - 1, 2 * RING, 3 * RING, 4 * RING)]
PREP_AT = {4: (7, 8, 9), 5: (10, 11), 6: (12, 13), 7: (14, 15)}
PREP2_AT = {9: (0, 1), 10: (2, 3)}
CLASS_SUM_AT = {2: (0,), 3: (1,), 4: (5,), 5: (6, 7, 8), 6: (9, 10, 11)}
HIDDEN_AT, CLASS_TURN_AT, CLASS_AT = 4, 7, 9
NETS_AT, NETS_TURN_AT, TURN_AT, BIAS_AT = (6, 7, 8), 9, 11, (13, 14, 15)
Y_MUL_AT = {False: (0, 2, 4, 6), True: (4, 5, 6, 7)}
Y_STATS_AT = {False: (1, 3, 5, 7), True: (4, 5, 6, 7)}
Y_NORM_AT = {False: (2, 4, 6, 8), True: (5, 6, 7, 8)}
PAD_COLS = ((0, 5, (CLS_HI, CLS_LO)), (5, 3, (SCL_HI, SCL_LO)))
NB = NETS * BATCHES


def build(nc, x, ids, pid, small, small_at, scales, rows, net_vecs, pw, W1s, W2s, int_W1, int_W2, out):
    f32, f32r, i32 = mybir.dt.float32, mybir.dt.float32r, mybir.dt.int32
    ACT = mybir.ActivationFunctionType
    AX = mybir.AxisListType

    x_v = x.rearrange("b (p t) d -> b p t d", t=TT)
    out_v = out.rearrange("b (p t) d -> b p t d", t=TT)

    with ExitStack() as ctx:
        def sb(name, shape, dt=f32):
            return ctx.enter_context(nc.sbuf_tensor(name, shape, dt))

        def sem(name):
            return ctx.enter_context(nc.semaphore(name))

        x_sb = sb("x_sb", [P, TT, D])
        xhat = sb("xhat", [P, TT, D])
        y_sb = sb("y_sb", [P, TT, D])
        pw_rows = sb("pw_rows", [P, TT, 2 * D])
        xbe = sb("xbe", [P, 2, TT, D])
        xT = sb("xT", [P, 2, TOKENS])
        v_sb = sb("v_sb", [P, 2, TOKENS])
        cat_hi = sb("cat_hi", [P, RING, TOKENS], f32r)
        cat_lo = sb("cat_lo", [P, RING, TOKENS], f32r)
        z_sb = sb("z_sb", [P, FT, TOKENS])
        with ExitStack() as prologue:
            def scratch(name, shape):
                return prologue.enter_context(nc.sbuf_tensor(name, shape, f32))
            net_rows = scratch("net_rows", [NB, 3, D])
            net_h = scratch("net_h", [NB, D])
            net_hidT = scratch("net_hidT", [P, NETS * FT, BATCHES])
            net_outT = scratch("net_outT", [P, FT, NB])
            mT = scratch("mT", [P, FT, NB])
            class_cols = scratch("class_cols", [P, FT, P])
        hid_hi = sb("hid_hi", [P, FT, TOKENS], f32r)
        hid_lo = sb("hid_lo", [P, FT, TOKENS], f32r)
        w1_hi = sb("w1_hi", [P, KT, D], f32r)
        w1_lo = sb("w1_lo", [P, KT, D], f32r)
        w2_hi = sb("w2_hi", [P, FT, D], f32r)
        w2_lo = sb("w2_lo", [P, FT, D], f32r)
        class_tab = sb("class_tab", [P, 3, D], f32r)
        class_bias = sb("class_bias", [P, D], f32r)
        onehot = sb("onehot", [P, TOKENS], f32r)
        ids_sb = sb("ids_sb", [P, TOKENS], i32)
        o_sb = sb("o_sb", [P, D])
        rows_bc = sb("rows_bc", [P, 3, D])
        b2_bc, g_bc, be_bc = [rows_bc[:, i, :] for i in range(3)]
        small_sb = sb("small_sb", [P, small.shape[1]])
        batch_bias = sb("batch_bias", [P, FT, BATCHES])
        pid_all = sb("pid_all", [P, BATCHES * TT], i32)
        pid_now = sb("pid_now", [P, TT], i32)
        w_tmp = sb("w_tmp", [P, 4])
        minus_half = sb("minus_half", [P, TT])
        eps_col = sb("eps_col", [P, TT])
        xst = sb("xst", [P, TT, 6])
        xmv = sb("xmv", [P, TT, 2])
        xve = sb("xve", [P, TT])
        xrs = sb("xrs", [P, TT])
        yst = sb("yst", [P, TT, 6])
        ymv = sb("ymv", [P, TT, 2])
        yve = sb("yve", [P, TT])
        yrs = sb("yrs", [P, TT])
        fst = sb("fst", [P, TT, 6])
        fmv = sb("fmv", [P, TT, 2])
        fve = sb("fve", [P, TT])
        frs = sb("frs", [P, TT])
        nst = sb("nst", [P, 6])
        nmv = sb("nmv", [P, 2])
        nrs = sb("nrs", [P, 2])
        def part(name, *dims):
            at, n = small_at[name]
            v = small_sb[:, at:at + n]
            return v.rearrange("p (a b) -> p a b", b=dims[0]) if dims else v

        w_mix, ident, cls_val = part("aw"), part("identity"), part("class_of")
        b1_cols, ib1_cols = part("b1T"), part("ib1T")
        sT, shifts = part("sT", BATCHES), part("shifts", 5)
        stage = [xbe[:, 1, i, :] for i in range(TT)] + [z_sb[:, 2, :], z_sb[:, 3, :]]
        tab_raw = y_sb[:, 0:3, :]

        hid_ps = ctx.enter_context(nc.psum_tensor("hid_ps", [P, FT, D], f32))
        t_ps = ctx.enter_context(nc.psum_tensor("t_ps", [P, TOKENS], f32))
        g_ps = ctx.enter_context(nc.psum_tensor("g_ps", [P, TOKENS], f32))
        o_ps = ctx.enter_context(nc.psum_tensor("o_ps", [P, 2, D], f32))

        small_in = sem("small_in")
        rows_bc_in = sem("rows_bc_in")
        pid_in = sem("pid_in")
        net_rows_in = sem("net_rows_in")
        stage_in = [sem(f"stage_in{i}") for i in range(STAGE)]
        pe_used = sem("pe_used")
        dve_used = sem("dve_used")
        act_began = sem("act_began")
        act_used = sem("act_used")
        w_hi_done = sem("w_hi_done")
        w_lo_done = sem("w_lo_done")
        sum_lo_done = sem("sum_lo_done")
        mix_max = sem("mix_max")
        mix_exp = sem("mix_exp")
        mix_ready = sem("mix_ready")
        tables_ready = sem("tables_ready")
        shifts_ready = sem("shifts_ready")
        net_silu = sem("net_silu")
        net_stats = sem("net_stats")
        net_ve = sem("net_ve")
        net_rs = sem("net_rs")
        net_copied = sem("net_copied")
        net_as_rows = sem("net_as_rows")
        m_rows = sem("m_rows")
        cols_cleared = sem("cols_cleared")
        cols_ready = sem("cols_ready")
        class_turned = sem("class_turned")
        tab_hi_done = sem("tab_hi_done")
        net_turned = sem("net_turned")
        mT_ready = sem("mT_ready")
        batch_bias_ready = sem("batch_bias_ready")
        class_bias_ready = sem("class_bias_ready")
        dve_chain = sem("dve_chain")
        half_ready = sem("half_ready")
        table_in = sem("table_in")
        x_in = sem("x_in")
        ids_in = sem("ids_in")
        rows_in = [sem(f"rows_in{t}") for t in range(TT)]
        pid_ready = sem("pid_ready")
        onehot_ready = sem("onehot_ready")
        xstat = sem("xstat")
        xaggr = sem("xaggr")
        xve_done = sem("xve_done")
        xrs_done = sem("xrs_done")
        xhat_done = sem("xhat_done")
        ymul = sem("ymul")
        yadd = sem("yadd")
        ystat = sem("ystat")
        yaggr = sem("yaggr")
        yve_done = sem("yve_done")
        yrs_done = sem("yrs_done")
        yhat_done = sem("yhat_done")
        fstat = sem("fstat")
        faggr = sem("faggr")
        fve_done = sem("fve_done")
        frs_done = sem("frs_done")
        o_done = sem("o_done")
        fnum = sem("fnum")
        out_ready = sem("out_ready")
        xbe_done = sem("xbe_done")
        tr_ready = sem("tr_ready")
        t_copied = sem("t_copied")
        x_hi_done = sem("x_hi_done")
        x_lo_done = sem("x_lo_done")
        picked = sem("picked")
        v_done = sem("v_done")
        m_hi_done = sem("m_hi_done")
        m_lo_done = sem("m_lo_done")
        first_done = sem("first_done")
        z_done = sem("z_done")
        hid_hi_done = sem("hid_hi_done")
        hid_lo_done = sem("hid_lo_done")
        second_done = sem("second_done")
        stored = [sem(f"stored{p}") for p in range(2)]
        last_stored = sem("last_stored")
        last_lo_done = sem("last_lo_done")

        def wait(eng, s, value):
            if not isinstance(value, int) or value > 0:
                eng.wait_ge(s, value)

        tiles = []

        def add(tensor, row, rows=P):
            tiles.append((tensor[row:row + rows, :], rows))
            return len(tiles) - 1

        SOURCE = {"h": 0, "t": 1, "s": 5}
        for k in range(FT):
            for j in (2, 3, 4):
                add(int_W1, j * D + k * P)
        MOD = []
        NET = []
        for i, (kind, f) in enumerate(ORDER[FT:]):
            if i == 6:
                NET += [add(W1s[0], c * P) for c in range(2)]
                NET += [add(W1s[n], 0, W1s[n].shape[0]) for n in (1, 2)]
            MOD.append(add(int_W1, SOURCE[kind] * D + f * P))
        NETW2 = len(tiles)
        for n in range(NETS):
            for k in range(FT):
                add(W2s[n], k * P)
        W2_0 = len(tiles)
        for k in range(FT):
            add(int_W2, k * P)
        BIAS0 = len(tiles)
        for k in range(FT):
            for j in (2, 3, 4):
                add(int_W1, j * D + k * P)

        PE_TILES = [n for n in range(NETS * FT, len(tiles)) if not W2_0 <= n < BIAS0]
        ACT_TILES = MOD + list(range(W2_0, BIAS0))

        def used(order, n):
            return order.index(n) + 1

        def stage_wait(eng, n):
            eng.wait_ge(stage_in[n % STAGE], 16 * (n // STAGE + 1))

        def released(eng, n):
            if n in PE_TILES:
                eng.wait_ge(pe_used, used(PE_TILES, n))
            if n in ACT_TILES:
                eng.wait_ge(act_used, used(ACT_TILES, n))
            if n < NETS * FT and n % NETS:
                eng.wait_ge(dve_used, n - n // NETS)
            if n < NETS * FT and n % NETS == 0:
                eng.wait_ge(act_began, n // NETS + 1)

        block = ctx.enter_context(nc.Block())

        @block.sync
        def _(sp):
            def load_x(b):
                wait(sp, tr_ready, TRS * (b - 1) + FT)
                wait(sp, xhat_done, TT * b)
                wait(sp, xbe_done, TT * b)
                sp.dma_start(x_sb[:, :, :], x_v[b]).then_inc(x_in, 16)

            def load_ids(b):
                wait(sp, onehot_ready, b)
                for half in range(2):
                    sp.dma_start(ids_sb[64 * half:64 * half + 64, :],
                                 ids[half, b].partition_broadcast(64)).then_inc(ids_in, 16)

            def store(b, par):
                sp.wait_ge(out_ready, TT * (b + 1))
                sp.dma_start(out_v[b], xbe[:, par]).then_inc(stored[par], 16)

            sp.dma_start(small_sb[:, :], small).then_inc(small_in, 16)
            for n, (src, rows_in_tile) in enumerate(tiles):
                if n == NETS:
                    sp.dma_start(x_sb[:, :, :], x_v[0]).then_inc(x_in, 16)
                if n == NETS * (FT - 1):
                    load_ids(0)
                    sp.dma_start(tab_raw, scales).then_inc(table_in, 16)
                    sp.dma_start(pid_all[:, :], pid).then_inc(pid_in, 16)
                if n == NETS * FT + 2:
                    sp.dma_start(rows_bc[:, :, :], rows.partition_broadcast(P)).then_inc(rows_bc_in, 16)
                if n == NETW2:
                    sp.dma_start(net_rows[:, :, :], net_vecs).then_inc(net_rows_in, 16)
                if n == NETW2 + 6:
                    load_x(1)
                    load_ids(1)
                if n >= STAGE:
                    released(sp, n - STAGE)
                sp.dma_start(stage[n % STAGE][0:rows_in_tile, :], src).then_inc(stage_in[n % STAGE], 16)

            def chunk(b, par, first=False, last=False):
                if not (first or last):
                    load_x(b + 1)
                    load_ids(b + 1)
                if not first:
                    store(b - 1, 1 - par)

            chunk(0, 0, first=True)
            with sp.Fori(0, BATCHES // 2 - 1) as pair:
                b = 2 * pair + 1
                chunk(b, 1)
                chunk(b + 1, 0)
            chunk(BATCHES - 1, 1, last=True)
            for t in range(TT):
                sp.wait_ge(out_ready, TT * (BATCHES - 1) + t + 1)
                sp.dma_start(out_v[BATCHES - 1, :, t, :], xbe[:, 1, t, :]).then_inc(last_stored, 16)
            sp.wait_ge(last_stored, 16 * TT)
            for par in range(2):
                sp.wait_ge(stored[par], 16 * (BATCHES // 2 - par))

        @block.gpsimd
        def _(pool):
            def rstd(stat_sem, count, ve, ve_sem, rs, rs_sem, mv, cols, nth):
                pool.wait_ge(stat_sem, count)
                pool.tensor_tensor(ve[:, cols], mv[:, cols, 1], eps_col[:, cols], ALU.add).then_inc(ve_sem, 1)
                pool.wait_ge(ve_sem, nth)
                pool.tensor_tensor(rs[:, cols], ve[:, cols], minus_half[:, cols], ALU.pow).then_inc(rs_sem, 1)

            def x_rstd(b):
                wait(pool, xhat_done, TT * b)
                rstd(xaggr, TT * (b + 1), xve, xve_done, xrs, xrs_done, xmv, slice(0, TT), b + 1)

            def add_be(b, par):
                wait(pool, stored[par], 8 * (b - par))
                wait(pool, x_in, 16 * (b + 1))
                for t in range(TT):
                    pool.tensor_tensor(xbe[:, par, t, :], x_sb[:, t, :], be_bc, ALU.add).then_inc(xbe_done, 1)

            def pid_copy(b):
                for t in range(TT):
                    wait(pool, rows_in[t], 16 * b)
                pool.tensor_copy(pid_now[:, :], pid_all[:, bass.ds(b * TT, TT)]).then_inc(pid_ready, 1)
                pool.wait_ge(pid_ready, b + 1)

            def gather(b, t):
                wait(pool, yadd, TT * (b - 1) + t + 1)
                pool.nop(nofuse=True)
                pool.indirect_dma_start(pw_rows[:, t, :], None, pw[:, :],
                                        bass.IndirectOffsetOnAxis(ap=pid_now[:, t:t + 1], axis=0)
                                        ).then_inc(rows_in[t], 16)

            def low_part(b, kk):
                n = MODS * b + MOD_BEFORE[kk]
                if ORDER[kk][0] == "x":
                    return
                pool.wait_ge(m_hi_done, n + 1)
                pool.tensor_tensor(cat_lo[:, kk % RING, :], v_sb[:, MOD_BEFORE[kk] % 2, :],
                                   cat_hi[:, kk % RING, :].bitcast(f32), ALU.subtract).then_inc(m_lo_done, 1)

            def hidden_low(b, h):
                pool.wait_ge(hid_hi_done, FT * b + h + 1)
                pool.tensor_tensor(hid_lo[:, h, :], z_sb[:, h, :], hid_hi[:, h, :].bitcast(f32),
                                   ALU.subtract).then_inc(hid_lo_done, 1)

            pool.memset(minus_half[:, :], -0.5).then_inc(half_ready, 1)
            pool.memset(eps_col[:, :], EPS).then_inc(half_ready, 1)
            pool.wait_ge(half_ready, 2)
            pool.memset(nrs[:, :], 0.0).then_inc(hid_lo_done, FT)
            pool.memset(class_cols[:, :, :], 0.0).then_inc(cols_cleared, 1)

            def sum_low(i):
                pool.wait_ge(w_hi_done, i + 1)
                pool.tensor_tensor(w1_lo[:, i, :], z_sb[:, i % 2, :], w1_hi[:, i, :].bitcast(f32),
                                   ALU.subtract).then_inc(sum_lo_done, 1)

            for i in range(FT - 1):
                sum_low(i)
            x_rstd(0)
            sum_low(FT - 1)
            pool.wait_ge(tab_hi_done, 1)
            pool.wait_ge(sum_lo_done, FT)
            for i, base in enumerate((CLS_LO, SCL_LO, CLS_LO)):
                rows = slice(base, base + 32)
                wait(pool, tables_ready, i)
                pool.tensor_tensor(class_tab[rows, i, :], tab_raw[rows, i, :],
                                   class_tab[rows, i, :].bitcast(f32), ALU.subtract).then_inc(tables_ready, 1)
            pool.wait_ge(tables_ready, 3)
            pool.wait_ge(pid_in, 16)
            pid_copy(0)
            for t in range(TT):
                gather(0, t)
            for kk in range(FT, FT + AHEAD):
                low_part(0, kk)

            def net_rstd():
                pool.wait_ge(net_stats, 1)
                pool.tensor_tensor(nrs[0:NB, 0:1], nmv[0:NB, 1:2], eps_col[0:NB, 0:1], ALU.add).then_inc(net_ve, 1)
                pool.wait_ge(net_ve, 1)
                pool.tensor_tensor(nrs[0:NB, 1:2], nrs[0:NB, 0:1], minus_half[0:NB, 0:1], ALU.pow).then_inc(net_rs, 1)

            def chunk(b, par, first=False, last=False):
                for k in range(KT):
                    kk = k + AHEAD
                    if first and kk < FT + AHEAD:
                        continue
                    if first and k == NETS_TURN_AT + 1:
                        net_rstd()
                    if kk < KT:
                        low_part(b, kk)
                    elif not last:
                        low_part(b + 1, kk - KT)
                    if not first and k < 2:
                        hidden_low(b - 1, 2 * k)
                        hidden_low(b - 1, 2 * k + 1)
                    if k in Y_STATS_AT[first]:
                        t = Y_STATS_AT[first].index(k)
                        rstd(yaggr, TT * b + t + 1, yve, yve_done, yrs, yrs_done, ymv, slice(t, t + 1), TT * b + t + 1)
                    if not first and k in (4, 6, 8, 10):
                        t = (k - 4) // 2
                        rstd(faggr, TT * (b - 1) + t + 1, fve, fve_done, frs, frs_done, fmv, slice(t, t + 1),
                             TT * (b - 1) + t + 1)
                    if not last:
                        if k == 8:
                            pid_copy(b + 1)
                        if k in (8, 9, 10, 11):
                            gather(b + 1, k - 8)
                        if k == 12:
                            x_rstd(b + 1)
                        if k == (15 if first else 14):
                            if first:
                                pool.wait_ge(act_used, MODS + FT)
                                pool.wait_ge(pe_used, len(PE_TILES))
                            add_be(b + 1, 1 - par)
                    if first and k == FT:
                        pool.wait_ge(rows_bc_in, 16)
                        add_be(0, 0)

            chunk(0, 0, first=True)
            with pool.Fori(0, BATCHES // 2 - 1) as pair:
                b = 2 * pair + 1
                chunk(b, 1)
                chunk(b + 1, 0)
            chunk(BATCHES - 1, 1, last=True)
            tail = BATCHES - 1
            for t in range(TT):
                rstd(faggr, TT * tail + t + 1, fve, fve_done, frs, frs_done, fmv, slice(t, t + 1),
                     TT * tail + t + 1)

        @block.scalar
        def _(act):
            act.wait_ge(mix_max, 1)
            act.activation(w_mix, w_mix, ACT.Exp, bias=w_tmp[:, 0:1]).then_inc(mix_exp, 1)
            act.wait_ge(mix_ready, 1)

            def begin_sum(i):
                n = NETS * i
                stage_wait(act, n)
                wait(act, sum_lo_done, i - 1)
                act.activation(z_sb[:, i % 2, :], stage[n % STAGE], ACT.Copy, scale=w_mix[:, 2:3]).then_inc(act_began, 1)

            def prepare(i, dst, n, scale):
                slot = z_sb[:, i % 2, :]
                if n is None:
                    act.wait_ge(dve_used, (NETS - 1) * (i + 1))
                else:
                    stage_wait(act, n)
                    if i < FT + 2:
                        act.wait_ge(sum_lo_done, i - 1)
                    else:
                        act.wait_ge(w_lo_done, i - 1 - FT)
                    act.activation(slot, stage[n % STAGE], ACT.Copy, scale=scale).then_inc(act_used, 1)
                    act.wait_ge(act_used, i - FT + 1)
                act.activation(dst, slot, ACT.Copy).then_inc(w_hi_done, 1)

            def prepare_w1(i):
                if i < FT:
                    prepare(i, w1_hi[:, i, :], None, None)
                else:
                    j = SOURCE[ORDER[i][0]]
                    prepare(i, w1_hi[:, i, :], MOD[i - FT], w_mix[:, j:j + 1])

            def prepare_w2(k):
                prepare(KT + k, w2_hi[:, k, :], W2_0 + k, 1.0)

            def nets_silu():
                act.wait_ge(pe_used, used(PE_TILES, NET[-1]))
                for i in range(NETS * FT):
                    act.activation(net_hidT[:, i, :], o_ps[:, 0, i * BATCHES:(i + 1) * BATCHES],
                                   ACT.Silu, bias=b1_cols[:, i:i + 1]).then_inc(net_silu, 1)

            def nets_copy():
                act.wait_ge(pe_used, used(PE_TILES, NETW2 + NETS * FT - 1))
                act.activation(net_outT[:, :, :].rearrange("p k b -> p (k b)"), o_ps[:, 0, 0:FT * NB],
                               ACT.Copy).then_inc(net_copied, 1)

            def make(b, kk):
                kind, f = ORDER[kk]
                if kind == "x":
                    act.wait_ge(tr_ready, TRS * b + TR_BEFORE[kk] + 1)
                    wait(act, first_done, FT * (KT * b + kk - RING + 1))
                    act.activation(cat_hi[:, kk % RING, :], t_ps[:, :], ACT.Copy).then_inc(x_hi_done, 1)
                    return
                if kind in "th":
                    act.wait_ge(tr_ready, TRS * b + TR_BEFORE[kk] + 1)
                    wait(act, v_done, MODS * b + MOD_BEFORE[kk] - (1 if (kind == "h") == (f > 0) and not (kind == "t" and f > 0) else 2))
                    act.activation(xT[:, NORM_BEFORE[kk] % 2, :], t_ps[:, :], ACT.Copy).then_inc(t_copied, 1)
                act.wait_ge(v_done, MODS * b + MOD_BEFORE[kk] + 1)
                wait(act, first_done, FT * (KT * b + kk - RING + 1))
                act.activation(cat_hi[:, kk % RING, :], v_sb[:, MOD_BEFORE[kk] % 2, :], ACT.Copy).then_inc(m_hi_done, 1)

            def hidden(b, h, tail=False):
                done = LAST_DONE[h] if tail else FT * (KT - 1) + h + 1
                act.wait_ge(first_done, FT * KT * b + done)
                act.wait_ge(hid_lo_done, FT * b + h + 1)
                act.activation(z_sb[:, h, :], hid_ps[:, h, :], ACT.Silu,
                               bias=batch_bias[:, h, bass.ds(b, 1)]).then_inc(z_done, 1)

            def hidden_high(b, h):
                act.wait_ge(z_done, FT * b + h + 1)
                act.wait_ge(second_done, TT * (b + 1))
                act.activation(hid_hi[:, h, :], z_sb[:, h, :], ACT.Copy).then_inc(hid_hi_done, 1)

            begin_sum(0)
            prepare_w1(0)
            begin_sum(1)
            make(0, 0)
            for kk in range(1, FT):
                if kk + 1 < FT:
                    begin_sum(kk + 1)
                else:
                    act.wait_ge(table_in, 16)
                    act.activation(class_tab[:, :, :], tab_raw, ACT.Copy).then_inc(tab_hi_done, 1)
                make(0, kk)
                prepare_w1(kk)
            for kk in range(FT, FT + AHEAD):
                prepare_w1(kk)
                make(0, kk)

            def chunk(b, first=False, last=False):
                for k in range(KT):
                    if first:
                        if k + AHEAD < FT + AHEAD:
                            continue
                        for i in PREP_AT.get(k, ()):
                            prepare_w1(i)
                        for i in PREP2_AT.get(k, ()):
                            prepare_w2(i)
                        if k == HIDDEN_AT + 1:
                            nets_silu()
                        if k == NETS_AT[-1] + 1:
                            nets_copy()
                    if not first and k == 0:
                        for h in range(FT):
                            hidden(b - 1, h)
                    kk = k + AHEAD
                    if kk < KT:
                        make(b, kk)
                    elif not last:
                        make(b + 1, kk - KT)
                    if not first and k < 2:
                        hidden_high(b - 1, 2 * k)
                        hidden_high(b - 1, 2 * k + 1)

            chunk(0, first=True)
            act.wait_ge(batch_bias_ready, FT)
            with act.Fori(0, BATCHES // 2 - 1) as pair:
                b = 2 * pair + 1
                chunk(b)
                chunk(b + 1)
            chunk(BATCHES - 1, last=True)
            for h in range(FT):
                hidden(BATCHES - 1, h, tail=True)

        @block.vector
        def _(dve):
            def x_stats(b, t):
                if t == 0:
                    dve.wait_ge(x_in, 16 * (b + 1))
                dve.bn_stats(xst[:, t, :], x_sb[:, t, :]).then_inc(xstat, 1)
                dve.wait_ge(xstat, TT * b + t + 1)
                dve.nop(nofuse=True)
                dve.bn_aggr(xmv[:, t, :], xst[:, t, :]).then_inc(xaggr, 1)

            def x_norm(b, t):
                dve.wait_ge(xrs_done, b + 1)
                if t == 0:
                    wait(dve, tr_ready, TRS * (b - 1) + TR_BEFORE[KT - FT])
                    wait(dve, ymul, TT * b)
                dve.tensor_scalar(xhat[:, t, :], x_sb[:, t, :], xmv[:, t, 0:1], xrs[:, t:t + 1],
                                  ALU.subtract, ALU.mult).then_inc(xhat_done, 1)

            def y_mul(b, t):
                dve.wait_ge(rows_in[t], 16 * (b + 1))
                dve.wait_ge(xhat_done, TT * (b + 1))
                wait(dve, tr_ready, TRS * b)
                if isinstance(b, int) and b == 0 and t == 0:
                    dve.wait_ge(tables_ready, 3)
                dve.tensor_tensor(y_sb[:, t, :], xhat[:, t, :], pw_rows[:, t, 0:D], ALU.mult).then_inc(ymul, 1)

            def y_add(b, t):
                n = TT * b + t + 1
                dve.wait_ge(ymul, n)
                dve.tensor_tensor(y_sb[:, t, :], y_sb[:, t, :], pw_rows[:, t, D:2 * D], ALU.add).then_inc(yadd, 1)
                dve.wait_ge(yadd, n)
                dve.bn_stats(yst[:, t, :], y_sb[:, t, :]).then_inc(ystat, 1)
                dve.wait_ge(ystat, n)
                dve.nop(nofuse=True)
                dve.bn_aggr(ymv[:, t, :], yst[:, t, :]).then_inc(yaggr, 1)

            def y_norm(b, t):
                dve.wait_ge(yrs_done, TT * b + t + 1)
                dve.tensor_scalar(y_sb[:, t, :], y_sb[:, t, :], ymv[:, t, 0:1], yrs[:, t:t + 1],
                                  ALU.subtract, ALU.mult).then_inc(yhat_done, 1)

            def compare(b):
                dve.wait_ge(ids_in, 32 * (b + 1))
                wait(dve, picked, MODS * b)
                dve.tensor_scalar(onehot[:, :], ids_sb[:, :], cls_val[:, 0:1], None, ALU.is_equal).then_inc(onehot_ready, 1)

            def make(b, kk):
                kind, f = ORDER[kk]
                if kind == "x":
                    dve.wait_ge(x_hi_done, FT * b + f + 1)
                    dve.tensor_tensor(cat_lo[:, kk % RING, :], t_ps[:, :], cat_hi[:, kk % RING, :].bitcast(f32),
                                      ALU.subtract).then_inc(x_lo_done, 1)
                    return
                n = MODS * b + MOD_BEFORE[kk]
                dve.wait_ge(t_copied, NORMS * b + NORM_BEFORE[kk] + (kind != "s"))
                dve.wait_ge(picked, n + 1)
                wait(dve, m_lo_done, n - 1)
                slot = (NORM_BEFORE[kk] - (kind == "s")) % 2
                dve.tensor_tensor(v_sb[:, MOD_BEFORE[kk] % 2, :], g_ps[:, :], xT[:, slot, :], ALU.mult).then_inc(v_done, 1)

            def out_stats(b, t):
                n = TT * b + t + 1
                dve.wait_ge(second_done, n + TT)
                wait(dve, out_ready, n - 1)
                dve.tensor_tensor(o_sb[:, :], o_ps[:, t % 2, :], b2_bc, ALU.add).then_inc(o_done, 1)
                dve.wait_ge(o_done, n + 1)
                dve.bn_stats(fst[:, t, :], o_sb[:, :]).then_inc(fstat, 1)
                dve.wait_ge(fstat, n)
                dve.nop(nofuse=True)
                dve.bn_aggr(fmv[:, t, :], fst[:, t, :]).then_inc(faggr, 1)
                dve.wait_ge(faggr, n)
                dve.scalar_tensor_tensor(o_sb[:, :], o_sb[:, :], fmv[:, t, 0:1], g_bc,
                                         ALU.subtract, ALU.mult).then_inc(fnum, 1)

            def out_sum(b, t, par):
                n = TT * b + t + 1
                dve.wait_ge(fnum, n)
                dve.wait_ge(frs_done, n)
                dve.wait_ge(xbe_done, n)
                dve.scalar_tensor_tensor(xbe[:, par, t, :], o_sb[:, :], frs[:, t:t + 1], xbe[:, par, t, :],
                                         ALU.mult, ALU.add).then_inc(out_ready, 1)

            def hidden_parts(b, h):
                dve.wait_ge(z_done, FT * b + h + 1)
                dve.wait_ge(second_done, TT * (b + 1))
                dve.tensor_copy(hid_hi[:, h, :], z_sb[:, h, :]).then_inc(hid_hi_done, 1)
                dve.wait_ge(hid_hi_done, FT * b + h + 1)
                dve.tensor_tensor(hid_lo[:, h, :], z_sb[:, h, :], hid_hi[:, h, :].bitcast(f32),
                                  ALU.subtract).then_inc(last_lo_done, 1)

            def link(ins):
                links[0] += 1
                ins.then_inc(dve_chain, 1)
                dve.wait_ge(dve_chain, links[0])

            def sum_blocks(i):
                v = z_sb[:, i % 2, :]
                dve.wait_ge(act_began, i + 1)
                for j in (1, 2):
                    n = NETS * i + j
                    stage_wait(dve, n)
                    dve.scalar_tensor_tensor(v, stage[n % STAGE], w_mix[:, 2 + j:3 + j], v,
                                             ALU.mult, ALU.add).then_inc(dve_used, 1)
                    dve.wait_ge(dve_used, (NETS - 1) * i + j)

            def prepare(i, dst_hi, dst_lo):
                v = z_sb[:, i % 2, :]
                dve.wait_ge(w_hi_done, i + 1)
                dve.tensor_tensor(dst_lo, v, dst_hi.bitcast(f32), ALU.subtract).then_inc(w_lo_done, 1)

            def prepare_w1(i):
                prepare(i, w1_hi[:, i, :], w1_lo[:, i, :])

            def prepare_w2(k):
                prepare(KT + k, w2_hi[:, k, :], w2_lo[:, k, :])

            def class_pad():
                dve.wait_ge(pe_used, used(PE_TILES, MOD[-1]))
                dve.wait_ge(cols_cleared, 1)
                sums = o_ps[:, 1, 0:FT * 8].rearrange("p (k c) -> p k c", c=8)
                for at, n_cls, bases in PAD_COLS:
                    for base in bases:
                        dve.tensor_copy(class_cols[:, :, base:base + n_cls], sums[:, :, at:at + n_cls]).then_inc(cols_ready, 1)

            def class_rows():
                dve.wait_ge(class_turned, 1)
                link(dve.tensor_copy(class_bias[:, :], o_ps[:, 1, :]))
                for base in (CLS_LO, SCL_LO):
                    rows = slice(base, base + 32)
                    dve.tensor_tensor(class_bias[rows, :], o_ps[rows, 1, :], class_bias[rows, :].bitcast(f32),
                                      ALU.subtract).then_inc(class_bias_ready, 1)

            def nets_stats():
                dve.wait_ge(net_as_rows, 1)
                dve.wait_ge(net_rows_in, 16)
                link(dve.tensor_tensor(net_h[:, :], o_ps[0:NB, 1, :], net_rows[:, 0, :], ALU.add))
                link(dve.bn_stats(nst[0:NB, :], net_h[:, :]))
                dve.bn_aggr(nmv[0:NB, :], nst[0:NB, :]).then_inc(net_stats, 1)

            def nets_norm():
                dve.wait_ge(net_rs, 1)
                link(dve.tensor_scalar(net_h[:, :], net_h[:, :], nmv[0:NB, 0:1], nrs[0:NB, 1:2],
                                       ALU.subtract, ALU.mult))
                link(dve.tensor_tensor(net_h[:, :], net_h[:, :], net_rows[:, 1, :], ALU.mult))
                dve.tensor_tensor(net_h[:, :], net_h[:, :], net_rows[:, 2, :], ALU.add).then_inc(m_rows, 1)

            def nets_weigh():
                dve.wait_ge(net_turned, 1)
                turned = o_ps[:, 0, 0:FT * NB].rearrange("p (k q) -> p k q", q=NB)
                for n in range(NETS):
                    cols = slice(BATCHES * n, BATCHES * (n + 1))
                    dve.tensor_scalar(mT[:, :, cols], turned[:, :, cols], w_mix[:, 2 + n:3 + n], None,
                                      ALU.mult).then_inc(mT_ready, 1)

            def add_b1():
                dve.wait_ge(pe_used, len(PE_TILES))
                for h in range(FT):
                    dve.tensor_scalar(batch_bias[:, h, :], o_ps[:, 1, h * BATCHES:(h + 1) * BATCHES],
                                      ib1_cols[:, h:h + 1], None, ALU.add).then_inc(batch_bias_ready, 1)

            links = [0]
            dve.wait_ge(small_in, 16)
            link(dve.reduce_max(w_tmp[:, 1:2], w_mix, AX.X))
            dve.tensor_scalar(w_tmp[:, 0:1], w_tmp[:, 1:2], -1.0, None, ALU.mult).then_inc(mix_max, 1)
            dve.wait_ge(mix_exp, 1)
            link(dve.reduce_sum(w_tmp[:, 2:3], w_mix, AX.X))
            link(dve.reciprocal(w_tmp[:, 3:4], w_tmp[:, 2:3]))
            dve.tensor_scalar(w_mix, w_mix, w_tmp[:, 3:4], None, ALU.mult).then_inc(mix_ready, 1)
            dve.wait_ge(mix_ready, 1)
            for i, j in enumerate((1, 5, 0)):
                dve.tensor_scalar(shifts[:, FT * i:FT * (i + 1), :], shifts[:, FT * i:FT * (i + 1), :],
                                  w_mix[:, j:j + 1], None, ALU.mult).then_inc(shifts_ready, 1)
            for kk in range(FT):
                sum_blocks(kk)
                make(0, kk)
                if kk == 2:
                    for t in range(TT):
                        x_stats(0, t)
            dve.memset(w_tmp[:, 0:1], 0.0).then_inc(o_done, 1)
            compare(0)
            for t in range(TT):
                x_norm(0, t)
            for kk in range(FT, FT + AHEAD):
                make(0, kk)
                prepare_w1(kk)

            def chunk(b, par, first=False, last=False):
                for k in range(KT):
                    kk = k + AHEAD
                    if first:
                        if kk < FT + AHEAD:
                            continue
                        for j in PREP_AT.get(k, ()):
                            prepare_w1(j)
                        for j in PREP2_AT.get(k, ()):
                            prepare_w2(j)
                        if k == CLASS_TURN_AT:
                            class_pad()
                        if k == CLASS_TURN_AT + 1:
                            class_rows()
                        if k == NETS_TURN_AT + 1:
                            nets_stats()
                        if k == TURN_AT:
                            nets_norm()
                        if k == TURN_AT + 1:
                            nets_weigh()
                    if kk < KT:
                        make(b, kk)
                    elif not last:
                        make(b + 1, kk - KT)
                    if k in Y_NORM_AT[first]:
                        y_norm(b, Y_NORM_AT[first].index(k))
                    if k in Y_MUL_AT[first]:
                        y_mul(b, Y_MUL_AT[first].index(k))
                    if k in Y_STATS_AT[first]:
                        y_add(b, Y_STATS_AT[first].index(k))
                    if not first and k in (4, 6, 8, 10):
                        out_stats(b - 1, (k - 4) // 2)
                    if not first and k in (5, 7, 9, 11):
                        out_sum(b - 1, (k - 5) // 2, 1 - par)
                    if not last:
                        if k in (8, 9, 10, 11):
                            x_stats(b + 1, k - 8)
                        if k == 13:
                            compare(b + 1)
                        if k in (14, 15):
                            x_norm(b + 1, 2 * (k - 14))
                            x_norm(b + 1, 2 * (k - 14) + 1)
                if first:
                    add_b1()

            chunk(0, 0, first=True)
            with dve.Fori(0, BATCHES // 2 - 1) as pair:
                b = 2 * pair + 1
                chunk(b, 1)
                chunk(b + 1, 0)
            chunk(BATCHES - 1, 1, last=True)
            for h in range(FT):
                hidden_parts(BATCHES - 1, h)
            for t in range(TT):
                out_stats(BATCHES - 1, t)
                out_sum(BATCHES - 1, t, 1)

        @block.tensor
        def _(pe):
            def shared_bank(out_at, lhsT, rhs, first_of_bank, last):
                for h in range(FT):
                    ins = pe.matmul(out_at(h), lhsT[:, h * P:(h + 1) * P], rhs,
                                    start=(first_of_bank and h == 0), stop=last, skip_group_check=True)
                return ins

            def class_sum(i):
                kind, f = ORDER[FT + i]
                at, n_cls = (5, 3) if kind == "s" else (0, 5)
                pe.wait_ge(shifts_ready, 3)
                stage_wait(pe, MOD[i])
                shared_bank(lambda h: o_ps[:, 1, 8 * h + at:8 * h + at + n_cls], stage[MOD[i] % STAGE],
                            shifts[:, FT * "tsh".index(kind) + f, 0:n_cls], i == 0,
                            i == MODS - 1).then_inc(pe_used, 1)

            def class_turn():
                pe.wait_ge(cols_ready, 4)
                for h in range(FT):
                    ins = pe.transpose(o_ps[:, 1, h * P:(h + 1) * P], class_cols[:, h, :], ident)
                ins.then_inc(class_turned, 1)

            def nets_hidden():
                for n in NET:
                    stage_wait(pe, n)
                for n in range(NETS):
                    parts = (0, 1) if n == 0 else (n + 1,)
                    for h in range(FT):
                        i = n * FT + h
                        for c in parts:
                            depth = tiles[NET[c]][1]
                            ins = pe.matmul(o_ps[:, 0, i * BATCHES:(i + 1) * BATCHES],
                                            stage[NET[c] % STAGE][0:depth, h * P:(h + 1) * P], sT[0:depth, c, :],
                                            start=(c == parts[0]), stop=(c == parts[-1]))
                            if n == NETS - 1 and h == FT - 1:
                                ins.then_inc(pe_used, len(NET))

            def nets_output(n):
                if n == 0:
                    pe.wait_ge(net_silu, NETS * FT)
                for k in range(FT):
                    i = FT * n + k
                    stage_wait(pe, NETW2 + i)
                    shared_bank(lambda h: o_ps[:, 0, NB * h + BATCHES * n:NB * h + BATCHES * (n + 1)],
                                stage[(NETW2 + i) % STAGE], net_hidT[:, i, :], i == 0,
                                i == NETS * FT - 1).then_inc(pe_used, 1)

            def nets_to_rows():
                pe.wait_ge(net_copied, 1)
                pe.wait_ge(class_bias_ready, 2)
                for k in range(FT):
                    ins = pe.transpose(o_ps[0:NB, 1, k * P:(k + 1) * P], net_outT[:, k, :], ident)
                ins.then_inc(net_as_rows, 1)

            def nets_turn():
                pe.wait_ge(m_rows, 1)
                for k in range(FT):
                    ins = pe.transpose(o_ps[:, 0, k * NB:(k + 1) * NB], net_h[:, k * P:(k + 1) * P], ident[0:NB, 0:NB])
                ins.then_inc(net_turned, 1)

            def batch_sum(part):
                if part == 0:
                    pe.wait_ge(mT_ready, NETS)
                for i in range(FT * part, FT * part + FT):
                    k, j = i // NETS, i % NETS
                    stage_wait(pe, BIAS0 + i)
                    shared_bank(lambda h: o_ps[:, 1, h * BATCHES:(h + 1) * BATCHES], stage[(BIAS0 + i) % STAGE],
                                mT[:, k, BATCHES * j:BATCHES * (j + 1)], i == 0,
                                i == NETS * FT - 1).then_inc(pe_used, 1)

            def make(b, kk):
                kind, f = ORDER[kk]
                if kind != "s":
                    if kind == "x" and f > 0:
                        pe.wait_ge(x_lo_done, FT * b + f)
                    elif kind == "t" and f == 0:
                        pe.wait_ge(x_lo_done, FT * (b + 1))
                    else:
                        wait(pe, t_copied, NORMS * b + NORM_BEFORE[kk])
                    if kind == "x":
                        pe.wait_ge(x_in, 16 * (b + 1))
                    elif f == 0:
                        pe.wait_ge(xhat_done if kind == "t" else yhat_done, TT * (b + 1))
                    src = {"x": x_sb, "t": xhat, "h": y_sb}[kind]
                    for t in range(TT):
                        ins = pe.transpose(t_ps[:, t * P:(t + 1) * P], src[:, t, f * P:(f + 1) * P], ident)
                    ins.then_inc(tr_ready, 1)
                if kind != "x":
                    wait(pe, v_done, MODS * b + MOD_BEFORE[kk])
                    pe.wait_ge(onehot_ready, b + 1)
                    if isinstance(b, int):
                        pe.wait_ge(tables_ready, 3)
                    pe.matmul(g_ps[:, :], class_tab[:, "tsh".index(kind), f * P:(f + 1) * P], onehot[:, :],
                              start=True, stop=True).then_inc(picked, 1)

            def first_ready(b, k, bias_last=False):
                if bias_last and k < FT:
                    pe.wait_ge(sum_lo_done, k + 1)
                elif bias_last:
                    pe.wait_ge(w_lo_done, k + 1 - FT)
                if k < FT:
                    pe.wait_ge(x_lo_done, FT * b + k + 1)
                else:
                    pe.wait_ge(m_lo_done, MODS * b + MOD_BEFORE[k] + 1)

            def first_part(k, h, start):
                hi, lo = cat_hi[:, k % RING, :], cat_lo[:, k % RING, :]
                cols = slice(h * P, (h + 1) * P)
                acc = hid_ps[:, h, :]
                pe.matmul(acc, w1_hi[:, k, cols], hi, start=start, stop=False)
                pe.matmul(acc, w1_hi[:, k, cols], lo, start=False, stop=False)
                pe.matmul(acc, w1_lo[:, k, cols], hi, start=False, stop=(k == KT - 1)).then_inc(first_done, 1)

            def first(b, k, bias_last=False):
                first_ready(b, k, bias_last)
                for h in range(FT):
                    if k == 0:
                        wait(pe, z_done, FT * (b - 1) + h + 1)
                    if k == (CLASS_AT if bias_last else 0):
                        pe.wait_ge(onehot_ready, b + 1)
                        pe.wait_ge(class_bias_ready, 2)
                        pe.matmul(hid_ps[:, h, :], class_bias[:, h * P:(h + 1) * P], onehot[:, :],
                                  start=(k == 0), stop=False)
                    first_part(k, h, start=(bias_last and k == 0))

            def second(b, t):
                pe.wait_ge(hid_lo_done, FT * (b + 2))
                pe.wait_ge(o_done, TT * b + t)
                for k in range(FT):
                    ins = second_part(o_ps[:, t % 2, :], t, k)
                ins.then_inc(second_done, 1)

            def second_part(acc, t, k):
                cols = slice(t * P, (t + 1) * P)
                pe.matmul(acc, hid_hi[:, k, cols], w2_hi[:, k, :], start=(k == 0), stop=False)
                pe.matmul(acc, hid_lo[:, k, cols], w2_hi[:, k, :], start=False, stop=False)
                return pe.matmul(acc, hid_hi[:, k, cols], w2_lo[:, k, :], start=False, stop=(k == FT - 1))

            def last_tiles(b):
                for k in range(KT - RING, KT - 1):
                    first_ready(b, k)
                    for h in (0, 1):
                        first_part(k, h, start=False)
                first_ready(b, KT - 1)
                for h in (0, 1):
                    first_part(KT - 1, h, start=False)
                for h in (2, 3):
                    for k in range(KT - RING, KT):
                        first_part(k, h, start=False)

            pe.wait_ge(small_in, 16)
            pe.transpose(g_ps[:, 0:P], ident, ident).then_inc(second_done, TT)
            make(0, 0)
            make(0, 1)

            def chunk(b, first_chunk=False, last=False):
                for k in range(KT):
                    kk = k + AHEAD
                    if first_chunk:
                        if k in BIAS_AT:
                            batch_sum(BIAS_AT.index(k))
                    if first_chunk and k < FT:
                        pass
                    elif kk < KT:
                        make(b, kk)
                    elif not last:
                        make(b + 1, kk - KT)
                    if first_chunk and k == NETS_TURN_AT:
                        nets_to_rows()
                    if last and k == KT - RING:
                        last_tiles(b)
                        return
                    first(b, k, bias_last=first_chunk)
                    if first_chunk:
                        if k + 2 < FT:
                            make(b, k + 2)
                        for i in CLASS_SUM_AT.get(k, ()):
                            class_sum(i)
                        if k == FT - 1:
                            for i in range(AHEAD):
                                make(b, FT + i)
                                class_sum(2 + i)
                        if k == HIDDEN_AT:
                            nets_hidden()
                        if k == CLASS_TURN_AT:
                            class_turn()
                        if k == TURN_AT:
                            nets_turn()
                        if k in NETS_AT:
                            nets_output(NETS_AT.index(k))
                    if not first_chunk and k in SECOND_AT:
                        second(b - 1, SECOND_AT[k])
                if first_chunk:
                    pe.wait_ge(w_lo_done, KT)

            chunk(0, first_chunk=True)
            with pe.Fori(0, BATCHES // 2 - 1) as pair:
                b = 2 * pair + 1
                chunk(b)
                chunk(b + 1)
            chunk(BATCHES - 1, last=True)
            for t in range(TT):
                pe.wait_ge(o_done, TT * (BATCHES - 1) + t)
                for k in range(FT):
                    pe.wait_ge(last_lo_done, k + 1)
                    ins = second_part(o_ps[:, t % 2, :], t, k)
                ins.then_inc(second_done, 1)


_NETS = ["mem", "noi", "res"]


def kernel(**inputs):
    import concourse.bacc as bacc
    from concourse.bass_utils import run_bass_kernel_spmd

    nc = bacc.Bacc("TRN2", target_bir_lowering=False, num_devices=1)
    arrays = {}

    def put(name, a):
        a = np.ascontiguousarray(a)
        arrays[name] = a
        return nc.dram_tensor(name, a.shape, mybir.dt.from_np(a.dtype), kind="ExternalInput").ap()

    def given(name):
        return np.asarray(inputs[name])

    def cond(name):
        return given("L0_cond_" + name)

    def by_column(ids):
        return ids.reshape(BATCHES, P, TT).transpose(0, 2, 1).reshape(BATCHES, TOKENS)

    def cols(v):
        return v.reshape(FT, P).T

    def turned(tab):
        t = tab.T.reshape(FT, P, -1).transpose(1, 0, 2)
        return np.pad(t, ((0, 0), (0, 0), (0, 5 - t.shape[2]))).reshape(P, -1)

    def features_first(v):
        t = v.T
        t = np.pad(t, ((0, -len(t) % P), (0, 0)))
        return t.reshape(-1, P, BATCHES).transpose(1, 0, 2).reshape(P, -1)

    class_of = np.full((P, 1), -1.0, np.float32)
    for base, n in ((CLS_HI, 5), (CLS_LO, 5), (SCL_HI, 3), (SCL_LO, 3)):
        class_of[base:base + n, 0] = np.arange(n)
    pieces = dict(
        aw=np.broadcast_to(cond("aw"), (P, 6)),
        identity=np.eye(P, dtype=np.float32),
        class_of=class_of,
        b1T=np.concatenate([cols(cond(n + "_b1")) for n in _NETS], axis=1),
        ib1T=cols(cond("int_b1")),
        sT=np.concatenate([features_first(given(n)) for n in ("cond_512", "cond_64", "fside_Bx32_0")], axis=1),
        shifts=np.concatenate([turned(cond(n)) for n in ("tm_b", "ms_b", "cp_b")], axis=1),
    )
    small_at, at = {}, 0
    for name, piece in pieces.items():
        small_at[name] = (at, piece.shape[1])
        at += piece.shape[1]
    scales = np.zeros((P, 3, D), np.float32)
    for i, (name, bases) in enumerate((("tm_g", (CLS_HI, CLS_LO)), ("ms_g", (SCL_HI, SCL_LO)),
                                       ("cp_g", (CLS_HI, CLS_LO)))):
        for base in bases:
            scales[base:base + len(cond(name)), i] = cond(name)
    net_vecs = np.stack([np.stack([cond(n + v) for v in ("_b2", "_g", "_be")]) for n in _NETS])
    cls, scl = given("itok_BxS_0_4"), given("mask_BxS_ik0")
    pathway = given("itok_BxS_0_999")
    args = dict(
        x=put("x", given("x")),
        ids=put("ids", np.stack([by_column(cls), by_column(scl)])),
        pid=put("pid", pathway.reshape(BATCHES, P, TT).transpose(1, 0, 2).reshape(P, BATCHES * TT)),
        small=put("small", np.concatenate(list(pieces.values()), axis=1)), small_at=small_at,
        scales=put("scales", scales),
        rows=put("rows", np.stack([cond("int_b2"), cond("int_g"), cond("int_be")])),
        net_vecs=put("net_vecs", np.repeat(net_vecs, BATCHES, axis=0)),
        pw=put("pw", np.concatenate([cond("pw_g"), cond("pw_b")], axis=1)),
        W1s=[put(n + "_W1", cond(n + "_W1")) for n in _NETS],
        W2s=[put(n + "_W2", cond(n + "_W2")) for n in _NETS],
        int_W1=put("int_W1", cond("int_W1")), int_W2=put("int_W2", cond("int_W2")),
        out=nc.dram_tensor("out", (BATCHES, TOKENS, D), mybir.dt.float32, kind="ExternalOutput").ap(),
    )
    build(nc, **args)
    r = run_bass_kernel_spmd(nc, [arrays], core_ids=[0])
    return r.results[0]["out"]
```

```python
from contextlib import ExitStack

import numpy as np
import concourse.bass as bass
from concourse import mybir
from concourse.alu_op_type import AluOpType as ALU

BATCHES, TOKENS, D = 16, 512, 512
P = 128
TT = TOKENS // P
FT = D // P
KT = 4 * FT
AHEAD = 3
RING = 4
STAGE = 6
EPS = 1e-5
NETS = 3
CLS_HI, CLS_LO, SCL_HI, SCL_LO = 0, 32, 64, 96

ORDER = [("x", f) for f in range(FT)]
for _f in range(FT):
    ORDER += [("t", _f), ("s", _f)]
ORDER += [("h", f) for f in range(FT)]
MOD_BEFORE = [sum(kind != "x" for kind, _ in ORDER[:k]) for k in range(KT + 1)]
PICK_BEFORE = [sum(kind in "ts" for kind, _ in ORDER[:k]) for k in range(KT + 1)]
TR_BEFORE = [sum(kind in "xh" for kind, _ in ORDER[:k]) for k in range(KT + 1)]
MODS, TRS, PICKS = MOD_BEFORE[KT], TR_BEFORE[KT], PICK_BEFORE[KT]
SECOND_AT = (5, 7, 9, 11)
OUT_AT = (6, 8, 10, 12)
SUM_AT = (7, 9, 11, 13)
LAST_DONE = [FT * (KT - RING) + n for n in (2 * RING - 1, 2 * RING, 3 * RING, 4 * RING)]
Y_MUL_AT = {False: (0, 1, 2, 3), True: (4, 4, 5, 5)}
Y_STATS_AT = {False: (1, 3, 5, 6), True: (4, 5, 6, 7)}
Y_NORM_AT = {False: (4, 6, 7, 8), True: (5, 6, 7, 8)}
X_NORM_AT = {False: (0, 2, 3, 5), True: (4, 6)}
GATHER_AT = (8, 9, 10, 11)

PREP_AT = {4: (7, 8, 9), 5: (10, 11), 6: (12, 13), 7: (14, 15)}
PREP2_AT = {9: (0, 1), 10: (2, 3)}
CLASS_SUM_AT = {2: (0, 1), 4: (5,), 5: (6, 7, 8), 6: (9, 10, 11)}
CLASS_AT = 9
HIDDEN_AT = 4
NET_OUTPUT_AT = {7: (0, 1, 2, 3), 8: (4, 5, 6, 7), 9: (8, 9, 10, 11)}
NORM_AT, TURN_AT = 11, 12
BATCH_SUM_AT = {13: (0, 1, 2, 3, 4, 5), 14: (6, 7, 8, 9, 10, 11)}
CLASS_OF = {"t": (5, (CLS_HI, CLS_LO)), "h": (5, (CLS_HI, CLS_LO)), "s": (3, (SCL_HI, SCL_LO))}
NB = NETS * BATCHES


def build(nc, x, ids, pid, small, small_at, scales, rows, net_vecs, pw, cp, W1s, W2s, int_W1, int_W2, out):
    f32, f32r, i32 = mybir.dt.float32, mybir.dt.float32r, mybir.dt.int32
    ACT = mybir.ActivationFunctionType
    AX = mybir.AxisListType

    x_v = x.rearrange("b (p t) d -> b p t d", t=TT)
    out_v = out.rearrange("b (p t) d -> b p t d", t=TT)

    stats_dram = nc.dram_tensor("token_stats", (P, 2 * TT), f32, kind="Internal").ap()

    with ExitStack() as ctx:
        def sb(name, shape, dt=f32):
            return ctx.enter_context(nc.sbuf_tensor(name, shape, dt))

        def sem(name):
            return ctx.enter_context(nc.semaphore(name))

        x_sb = sb("x_sb", [P, TT, D])
        y_sb = sb("y_sb", [P, TT, D])
        pw_rows = sb("pw_rows", [P, TT, 2 * D])
        xbe = sb("xbe", [P, 2, TT, D])
        xhatT = sb("xhatT", [P, FT, TOKENS])
        stats_bc = sb("stats_bc", [P, P, 2, TT])
        v_sb = sb("v_sb", [P, 2, TOKENS])
        cat_hi = sb("cat_hi", [P, RING, TOKENS], f32r)
        cat_lo = sb("cat_lo", [P, RING, TOKENS], f32r)
        z_sb = sb("z_sb", [P, FT, TOKENS])
        with ExitStack() as prologue:
            def scratch(name, shape):
                return prologue.enter_context(nc.sbuf_tensor(name, shape, f32))
            class_cols = scratch("class_cols", [P, MODS, P])
            net_rows = class_cols[0:NB, :, :].rearrange("b m c -> b (m c)").rearrange("b (v d) -> b v d", v=3)
            net_h = scratch("net_h", [NB, D])
            net_hidT = scratch("net_hidT", [P, NETS * FT, NB])
            mT = scratch("mT", [P, FT, NB])
        hid_hi = sb("hid_hi", [P, FT, TOKENS], f32r)
        hid_lo = sb("hid_lo", [P, FT, TOKENS], f32r)
        w1_hi = sb("w1_hi", [P, KT, D], f32r)
        w1_lo = sb("w1_lo", [P, KT, D], f32r)
        w2_hi = sb("w2_hi", [P, FT, D], f32r)
        w2_lo = sb("w2_lo", [P, FT, D], f32r)
        class_tab = sb("class_tab", [P, 2, D], f32r)
        class_bias = sb("class_bias", [P, D], f32r)
        onehot = sb("onehot", [P, TOKENS], f32r)
        ids_sb = sb("ids_sb", [P, TOKENS], i32)
        o_sb = sb("o_sb", [P, D])
        rows_bc = sb("rows_bc", [P, 3, D])
        b2_bc, g_bc, be_bc = [rows_bc[:, i, :] for i in range(3)]
        small_sb = sb("small_sb", [P, small.shape[1]])
        batch_bias = sb("batch_bias", [P, FT, BATCHES])
        row_ids = sb("row_ids", [P, BATCHES * 2 * TT], i32)
        row_ids_now = sb("row_ids_now", [P, 2 * TT], i32)
        w_tmp = sb("w_tmp", [P, 4])
        minus_half = sb("minus_half", [P, TT])
        eps_col = sb("eps_col", [P, TT])
        xst = sb("xst", [P, TT, 6])
        xmv = sb("xmv", [P, TT, 2])
        xve = sb("xve", [P, TT])
        x_pack = sb("x_pack", [P, 2, TT])
        xrs = x_pack[:, 1, :]
        yst = sb("yst", [P, TT, 6])
        ymv = sb("ymv", [P, TT, 2])
        yve = sb("yve", [P, TT])
        yrs = sb("yrs", [P, TT])
        fst = sb("fst", [P, TT, 6])
        fmv = sb("fmv", [P, TT, 2])
        fve = sb("fve", [P, TT])
        frs = sb("frs", [P, TT])
        nst = sb("nst", [P, 6])
        nmv = sb("nmv", [P, 2])
        nrs = sb("nrs", [P, 2])

        def part(name, *dims):
            at, n = small_at[name]
            v = small_sb[:, at:at + n]
            return v.rearrange("p (a b) -> p a b", b=dims[0]) if dims else v

        w_mix, ident, cls_val = part("aw"), part("identity"), part("class_of")
        b1_cols, ib1_cols = part("b1T"), part("ib1T")
        sT, shifts = part("sT", BATCHES), part("shifts", 5)
        stage = [xbe[:, 1, i, :] for i in range(TT)] + [z_sb[:, 2, :], z_sb[:, 3, :]]
        tab_raw = y_sb[:, 0:2, :]

        hid_ps = ctx.enter_context(nc.psum_tensor("hid_ps", [P, FT, D], f32))
        made_ps = ctx.enter_context(nc.psum_tensor("made_ps", [P, 2, TOKENS], f32))
        o_ps = ctx.enter_context(nc.psum_tensor("o_ps", [P, 2, D], f32))

        small_in = sem("small_in")
        rows_bc_in = sem("rows_bc_in")
        row_ids_in = sem("row_ids_in")
        net_rows_in = sem("net_rows_in")
        stage_in = [sem(f"stage_in{i}") for i in range(STAGE)]
        pe_used = sem("pe_used")
        dve_used = sem("dve_used")
        act_began = sem("act_began")
        act_used = sem("act_used")
        w_hi_done = sem("w_hi_done")
        w_lo_done = sem("w_lo_done")
        sum_lo_done = sem("sum_lo_done")
        mix_max = sem("mix_max")
        mix_exp = sem("mix_exp")
        mix_ready = sem("mix_ready")
        tables_ready = sem("tables_ready")
        shifts_ready = sem("shifts_ready")
        net_silu = sem("net_silu")
        net_stats = sem("net_stats")
        net_ve = sem("net_ve")
        net_rs = sem("net_rs")
        m_rows = sem("m_rows")
        cols_cleared = sem("cols_cleared")
        tab_hi_done = sem("tab_hi_done")
        net_turned = sem("net_turned")
        batch_rows = sem("batch_rows")
        batch_turned = sem("batch_turned")
        mT_ready = sem("mT_ready")
        batch_bias_ready = sem("batch_bias_ready")
        class_bias_ready = sem("class_bias_ready")
        dve_chain = sem("dve_chain")
        half_ready = sem("half_ready")
        table_in = sem("table_in")
        x_in = sem("x_in")
        ids_in = sem("ids_in")
        rows_in = [sem(f"rows_in{t}") for t in range(TT)]
        class_rows_in = [sem(f"class_rows_in{t}") for t in range(TT)]
        row_ids_ready = sem("row_ids_ready")
        onehot_ready = sem("onehot_ready")
        xstat = sem("xstat")
        xaggr = sem("xaggr")
        xve_done = sem("xve_done")
        xrs_done = sem("xrs_done")
        x_packed = sem("x_packed")
        stats_in = sem("stats_in")
        x_kept = sem("x_kept")
        centred = sem("centred")
        xhat_done = sem("xhat_done")
        ymul = sem("ymul")
        yadd = sem("yadd")
        ystat = sem("ystat")
        yaggr = sem("yaggr")
        yve_done = sem("yve_done")
        yrs_done = sem("yrs_done")
        yscaled = sem("yscaled")
        yhat_done = sem("yhat_done")
        fstat = sem("fstat")
        faggr = sem("faggr")
        fve_done = sem("fve_done")
        frs_done = sem("frs_done")
        o_done = sem("o_done")
        fnum = sem("fnum")
        out_ready = sem("out_ready")
        xbe_done = sem("xbe_done")
        tr_ready = sem("tr_ready")
        t_copied = sem("t_copied")
        x_hi_done = sem("x_hi_done")
        x_lo_done = sem("x_lo_done")
        picked = sem("picked")
        v_done = sem("v_done")
        m_hi_done = sem("m_hi_done")
        m_lo_done = sem("m_lo_done")
        first_done = sem("first_done")
        z_done = sem("z_done")
        hid_hi_done = sem("hid_hi_done")
        hid_lo_done = sem("hid_lo_done")
        second_done = sem("second_done")
        stored = [sem(f"stored{p}") for p in range(2)]
        last_stored = sem("last_stored")
        last_lo_done = sem("last_lo_done")

        def wait(eng, s, value):
            if not isinstance(value, int) or value > 0:
                eng.wait_ge(s, value)

        tiles = []

        def add(tensor, row, rows=P):
            tiles.append((tensor[row:row + rows, :], rows))
            return len(tiles) - 1

        SOURCE = {"h": 0, "t": 1, "s": 5}
        for k in range(FT):
            for j in (2, 3, 4):
                add(int_W1, j * D + k * P)
        MOD, NET = [], []
        for i, (kind, f) in enumerate(ORDER[FT:]):
            if i == 6:
                NET += [add(W1s[0], c * P) for c in range(2)]
                NET += [add(W1s[n], 0, W1s[n].shape[0]) for n in (1, 2)]
            MOD.append(add(int_W1, SOURCE[kind] * D + f * P))
        NETW2 = len(tiles)
        for n in range(NETS):
            for k in range(FT):
                add(W2s[n], k * P)
        W2_0 = len(tiles)
        for k in range(FT):
            add(int_W2, k * P)
        BIAS0 = len(tiles)
        for k in range(FT):
            for j in (2, 3, 4):
                add(int_W1, j * D + k * P)

        PE_TILES = [n for n in range(NETS * FT, len(tiles)) if not W2_0 <= n < BIAS0]
        ACT_TILES = MOD + list(range(W2_0, BIAS0))

        def used(order, n):
            return order.index(n) + 1

        def stage_wait(eng, n):
            eng.wait_ge(stage_in[n % STAGE], 16 * (n // STAGE + 1))

        def released(eng, n):
            if n in PE_TILES:
                eng.wait_ge(pe_used, used(PE_TILES, n))
            if n in ACT_TILES:
                eng.wait_ge(act_used, used(ACT_TILES, n))
            if n < NETS * FT and n % NETS:
                eng.wait_ge(dve_used, n - n // NETS)
            if n < NETS * FT and n % NETS == 0:
                eng.wait_ge(act_began, n // NETS + 1)

        block = ctx.enter_context(nc.Block())

        @block.sync
        def _(sp):
            def load_x(b):
                wait(sp, tr_ready, TRS * (b - 1) + FT)
                wait(sp, ymul, TT * b)
                wait(sp, xbe_done, TT * b)
                sp.dma_start(x_sb[:, :, :], x_v[b]).then_inc(x_in, 16)

            def load_ids(b):
                wait(sp, onehot_ready, b)
                for half in range(2):
                    sp.dma_start(ids_sb[64 * half:64 * half + 64, :],
                                 ids[half, b].partition_broadcast(64)).then_inc(ids_in, 16)

            def store(b, par):
                sp.wait_ge(out_ready, TT * (b + 1))
                sp.dma_start(out_v[b], xbe[:, par]).then_inc(stored[par], 16)

            sp.dma_start(small_sb[:, :], small).then_inc(small_in, 16)
            for n, (src, rows_in_tile) in enumerate(tiles):
                if n == NETS:
                    sp.dma_start(x_sb[:, :, :], x_v[0]).then_inc(x_in, 16)
                if n == NETS * (FT - 1):
                    load_ids(0)
                    sp.dma_start(tab_raw, scales).then_inc(table_in, 16)
                    sp.dma_start(row_ids[:, :], pid).then_inc(row_ids_in, 16)
                if n == NETS * FT + 2:
                    sp.dma_start(rows_bc[:, :, :], rows.partition_broadcast(P)).then_inc(rows_bc_in, 16)
                if n == NETW2 + STAGE + 1:
                    sp.wait_ge(pe_used, used(PE_TILES, MOD[-1]))
                    sp.dma_start(net_rows, net_vecs).then_inc(net_rows_in, 16)
                if n == NETW2 + 6:
                    load_x(1)
                    load_ids(1)
                if n >= STAGE:
                    released(sp, n - STAGE)
                sp.dma_start(stage[n % STAGE][0:rows_in_tile, :], src).then_inc(stage_in[n % STAGE], 16)

            def chunk(b, par, first=False, last=False):
                if not (first or last):
                    load_x(b + 1)
                    load_ids(b + 1)
                if not first:
                    store(b - 1, 1 - par)

            chunk(0, 0, first=True)
            with sp.Fori(0, BATCHES // 2 - 1) as pair:
                b = 2 * pair + 1
                chunk(b, 1)
                chunk(b + 1, 0)
            chunk(BATCHES - 1, 1, last=True)
            for t in range(TT):
                sp.wait_ge(out_ready, TT * (BATCHES - 1) + t + 1)
                sp.dma_start(out_v[BATCHES - 1, :, t, :], xbe[:, 1, t, :]).then_inc(last_stored, 16)
            sp.wait_ge(last_stored, 16 * TT)
            for par in range(2):
                sp.wait_ge(stored[par], 16 * (BATCHES // 2 - par))

        @block.gpsimd
        def _(pool):
            def rstd(stat_sem, count, ve, ve_sem, rs, rs_sem, mv, cols, nth):
                pool.wait_ge(stat_sem, count)
                pool.tensor_tensor(ve[:, cols], mv[:, cols, 1], eps_col[:, cols], ALU.add).then_inc(ve_sem, 1)
                pool.wait_ge(ve_sem, nth)
                pool.tensor_tensor(rs[:, cols], ve[:, cols], minus_half[:, cols], ALU.pow).then_inc(rs_sem, 1)

            def x_rstd(b):
                pool.wait_ge(xaggr, TT * (b + 1))
                pool.nop(nofuse=True)
                pool.tensor_copy(x_pack[:, 0, :], xmv[:, :, 0]).then_inc(xve_done, 1)
                rstd(xaggr, TT * (b + 1), xve, xve_done, xrs, xrs_done, xmv, slice(0, TT), 2 * (b + 1))
                pool.wait_ge(xrs_done, b + 1)
                pool.nop(nofuse=True)
                pool.dma_start(stats_dram, x_pack[:, :, :].rearrange("p s t -> p (s t)")).then_inc(x_packed, 16)

            def x_spread(b):
                wait(pool, xhat_done, FT * b)
                pool.wait_ge(x_packed, 16 * (b + 1))
                pool.nop(nofuse=True)
                pool.dma_start(stats_bc[:, :, :, :].rearrange("q p s t -> q (p s t)"),
                               stats_dram.rearrange("p c -> (p c)").partition_broadcast(P)).then_inc(stats_in, 16)

            def add_be(b, par):
                wait(pool, stored[par], 8 * (b - par))
                wait(pool, x_in, 16 * (b + 1))
                for t in range(TT):
                    pool.tensor_tensor(xbe[:, par, t, :], x_sb[:, t, :], be_bc, ALU.add).then_inc(xbe_done, 1)

            def ids_now(b):
                for t in range(TT):
                    wait(pool, rows_in[t], 16 * b)
                    wait(pool, class_rows_in[t], 16 * b)
                pool.tensor_copy(row_ids_now[:, :], row_ids[:, bass.ds(b * 2 * TT, 2 * TT)]).then_inc(row_ids_ready, 1)
                pool.wait_ge(row_ids_ready, b + 1)

            def gather(b, t):
                wait(pool, yscaled, TT * (b - 1) + t + 1)
                pool.nop(nofuse=True)
                pool.indirect_dma_start(pw_rows[:, t, :], None, pw[:, :],
                                        bass.IndirectOffsetOnAxis(ap=row_ids_now[:, t:t + 1], axis=0)
                                        ).then_inc(rows_in[t], 16)

            def gather_class(b, t):
                pool.wait_ge(ymul, TT * b + t + 1)
                pool.nop(nofuse=True)
                pool.indirect_dma_start(pw_rows[:, t, 0:D], None, cp[:, :],
                                        bass.IndirectOffsetOnAxis(ap=row_ids_now[:, TT + t:TT + t + 1], axis=0)
                                        ).then_inc(class_rows_in[t], 16)

            def low_part(b, kk):
                n = MODS * b + MOD_BEFORE[kk]
                if ORDER[kk][0] == "x":
                    return
                pool.wait_ge(m_hi_done, n + 1)
                pool.tensor_tensor(cat_lo[:, kk % RING, :], v_sb[:, MOD_BEFORE[kk] % 2, :],
                                   cat_hi[:, kk % RING, :].bitcast(f32), ALU.subtract).then_inc(m_lo_done, 1)

            def hidden_low(b, h):
                pool.wait_ge(hid_hi_done, FT * b + h + 1)
                pool.tensor_tensor(hid_lo[:, h, :], z_sb[:, h, :], hid_hi[:, h, :].bitcast(f32),
                                   ALU.subtract).then_inc(hid_lo_done, 1)

            pool.memset(minus_half[:, :], -0.5).then_inc(half_ready, 1)
            pool.memset(eps_col[:, :], EPS).then_inc(half_ready, 1)
            pool.wait_ge(half_ready, 2)
            pool.memset(nrs[:, :], 0.0).then_inc(hid_lo_done, FT)
            pool.memset(class_cols[:, :, :], 0.0).then_inc(cols_cleared, 1)
            pool.memset(net_hidT[:, :, :], 0.0).then_inc(cols_cleared, 1)

            def sum_low(i):
                pool.wait_ge(w_hi_done, i + 1)
                pool.tensor_tensor(w1_lo[:, i, :], z_sb[:, i % 2, :], w1_hi[:, i, :].bitcast(f32),
                                   ALU.subtract).then_inc(sum_lo_done, 1)

            for i in range(FT):
                sum_low(i)
                if i == 1:
                    x_rstd(0)
            x_spread(0)
            pool.wait_ge(tab_hi_done, 1)
            pool.wait_ge(sum_lo_done, FT)
            for i, base in enumerate((CLS_LO, SCL_LO)):
                rows = slice(base, base + 32)
                wait(pool, tables_ready, i)
                pool.tensor_tensor(class_tab[rows, i, :], tab_raw[rows, i, :],
                                   class_tab[rows, i, :].bitcast(f32), ALU.subtract).then_inc(tables_ready, 1)
            pool.wait_ge(tables_ready, 2)
            pool.wait_ge(row_ids_in, 16)
            ids_now(0)
            gather(0, 0)
            for t in range(1, TT):
                gather(0, t)
                low_part(0, FT + t - 1)

            def net_rstd():
                pool.wait_ge(net_stats, 1)
                pool.tensor_tensor(nrs[0:NB, 0:1], nmv[0:NB, 1:2], eps_col[0:NB, 0:1], ALU.add).then_inc(net_ve, 1)
                pool.wait_ge(net_ve, 1)
                pool.tensor_tensor(nrs[0:NB, 1:2], nrs[0:NB, 0:1], minus_half[0:NB, 0:1], ALU.pow).then_inc(net_rs, 1)

            def chunk(b, par, first=False, last=False):
                for k in range(KT):
                    kk = k + AHEAD
                    if first and kk < FT + AHEAD:
                        continue
                    if first and k == NORM_AT - 1:
                        net_rstd()
                    if kk < KT:
                        low_part(b, kk)
                    elif not last:
                        low_part(b + 1, kk - KT)
                    if not first and k < 2:
                        hidden_low(b - 1, 2 * k)
                        hidden_low(b - 1, 2 * k + 1)
                    for t in range(TT):
                        if Y_MUL_AT[first][t] == k:
                            gather_class(b, t)
                    if k in Y_STATS_AT[first]:
                        t = Y_STATS_AT[first].index(k)
                        rstd(yaggr, TT * b + t + 1, yve, yve_done, yrs, yrs_done, ymv, slice(t, t + 1), TT * b + t + 1)
                    if not first and k in OUT_AT:
                        t = OUT_AT.index(k)
                        rstd(faggr, TT * (b - 1) + t + 1, fve, fve_done, frs, frs_done, fmv, slice(t, t + 1),
                             TT * (b - 1) + t + 1)
                    if not last:
                        if k == 8:
                            ids_now(b + 1)
                        if k in GATHER_AT:
                            gather(b + 1, GATHER_AT.index(k))
                        if k == 12:
                            x_rstd(b + 1)
                        if k == 13:
                            x_spread(b + 1)
                        if k == KT - 1:
                            if first:
                                pool.wait_ge(act_used, MODS + FT)
                                pool.wait_ge(pe_used, len(PE_TILES))
                            add_be(b + 1, 1 - par)
                    if first and k == FT:
                        pool.wait_ge(rows_bc_in, 16)
                        add_be(0, 0)

            chunk(0, 0, first=True)
            with pool.Fori(0, BATCHES // 2 - 1) as pair:
                b = 2 * pair + 1
                chunk(b, 1)
                chunk(b + 1, 0)
            chunk(BATCHES - 1, 1, last=True)
            tail = BATCHES - 1
            for t in range(TT):
                rstd(faggr, TT * tail + t + 1, fve, fve_done, frs, frs_done, fmv, slice(t, t + 1),
                     TT * tail + t + 1)

        @block.scalar
        def _(act):
            act.wait_ge(mix_max, 1)
            act.activation(w_mix, w_mix, ACT.Exp, bias=w_tmp[:, 0:1]).then_inc(mix_exp, 1)
            act.wait_ge(mix_ready, 1)

            def begin_sum(i):
                n = NETS * i
                stage_wait(act, n)
                wait(act, sum_lo_done, i - 1)
                act.activation(z_sb[:, i % 2, :], stage[n % STAGE], ACT.Copy, scale=w_mix[:, 2:3]).then_inc(act_began, 1)

            def prepare(i, dst, n, scale):
                slot = z_sb[:, i % 2, :]
                if n is None:
                    act.wait_ge(dve_used, (NETS - 1) * (i + 1))
                else:
                    stage_wait(act, n)
                    if i < FT + 2:
                        act.wait_ge(sum_lo_done, i - 1)
                    else:
                        act.wait_ge(w_lo_done, i - 1 - FT)
                    act.activation(slot, stage[n % STAGE], ACT.Copy, scale=scale).then_inc(act_used, 1)
                    act.wait_ge(act_used, i - FT + 1)
                act.activation(dst, slot, ACT.Copy).then_inc(w_hi_done, 1)

            def prepare_w1(i):
                if i < FT:
                    prepare(i, w1_hi[:, i, :], None, None)
                else:
                    j = SOURCE[ORDER[i][0]]
                    prepare(i, w1_hi[:, i, :], MOD[i - FT], w_mix[:, j:j + 1])

            def prepare_w2(k):
                prepare(KT + k, w2_hi[:, k, :], W2_0 + k, 1.0)

            def nets_silu():
                act.wait_ge(pe_used, used(PE_TILES, NET[-1]))
                act.wait_ge(cols_cleared, 2)
                for i in range(NETS * FT):
                    n = i // FT
                    act.activation(net_hidT[:, i, n * BATCHES:(n + 1) * BATCHES], o_ps[:, 0, i * BATCHES:(i + 1) * BATCHES],
                                   ACT.Silu, bias=b1_cols[:, i:i + 1]).then_inc(net_silu, 1)

            def make(b, kk):
                kind, f = ORDER[kk]
                if kind == "x":
                    act.wait_ge(tr_ready, TRS * b + TR_BEFORE[kk] + 1)
                    wait(act, first_done, FT * (KT * b + kk - RING + 1))
                    act.activation(cat_hi[:, kk % RING, :], made_ps[:, kk % 2, :], ACT.Copy).then_inc(x_hi_done, 1)
                    wait(act, v_done, PICKS * b)
                    act.activation(xhatT[:, f, :], made_ps[:, kk % 2, :], ACT.Copy).then_inc(x_kept, 1)
                    return
                n = MODS * b + MOD_BEFORE[kk]
                slot = v_sb[:, MOD_BEFORE[kk] % 2, :]
                if kind == "h":
                    act.wait_ge(tr_ready, TRS * b + TR_BEFORE[kk] + 1)
                    act.wait_ge(m_lo_done, n - 1)
                    act.activation(slot, made_ps[:, kk % 2, :], ACT.Copy).then_inc(t_copied, 1)
                    act.wait_ge(t_copied, FT * b + f + 1)
                else:
                    act.wait_ge(v_done, PICKS * b + PICK_BEFORE[kk] + 1)
                wait(act, first_done, FT * (KT * b + kk - RING + 1))
                act.activation(cat_hi[:, kk % RING, :], slot, ACT.Copy).then_inc(m_hi_done, 1)

            def hidden(b, h, tail=False):
                done = LAST_DONE[h] if tail else FT * (KT - 1) + h + 1
                act.wait_ge(first_done, FT * KT * b + done)
                act.wait_ge(hid_lo_done, FT * b + h + 1)
                act.activation(z_sb[:, h, :], hid_ps[:, h, :], ACT.Silu,
                               bias=batch_bias[:, h, bass.ds(b, 1)]).then_inc(z_done, 1)

            def hidden_high(b, h):
                act.wait_ge(z_done, FT * b + h + 1)
                act.wait_ge(second_done, TT * (b + 1))
                act.activation(hid_hi[:, h, :], z_sb[:, h, :], ACT.Copy).then_inc(hid_hi_done, 1)

            begin_sum(0)
            prepare_w1(0)
            begin_sum(1)
            make(0, 0)
            for kk in range(1, FT):
                if kk + 1 < FT:
                    begin_sum(kk + 1)
                else:
                    act.wait_ge(table_in, 16)
                    act.activation(class_tab[:, :, :], tab_raw, ACT.Copy).then_inc(tab_hi_done, 1)
                make(0, kk)
                prepare_w1(kk)
            for kk in range(FT, FT + AHEAD):
                prepare_w1(kk)
                make(0, kk)

            def chunk(b, first=False, last=False):
                for k in range(KT):
                    if first:
                        if k + AHEAD < FT + AHEAD:
                            continue
                        for i in PREP_AT.get(k, ()):
                            prepare_w1(i)
                        for i in PREP2_AT.get(k, ()):
                            prepare_w2(i)
                        if k == HIDDEN_AT + 1:
                            nets_silu()
                    if not first and k == 0:
                        for h in range(FT):
                            hidden(b - 1, h)
                    kk = k + AHEAD
                    if kk < KT:
                        make(b, kk)
                    elif not last:
                        make(b + 1, kk - KT)
                    if not first and k < 2:
                        hidden_high(b - 1, 2 * k)
                        hidden_high(b - 1, 2 * k + 1)

            chunk(0, first=True)
            act.wait_ge(batch_bias_ready, FT)
            with act.Fori(0, BATCHES // 2 - 1) as pair:
                b = 2 * pair + 1
                chunk(b)
                chunk(b + 1)
            chunk(BATCHES - 1, last=True)
            for h in range(FT):
                hidden(BATCHES - 1, h, tail=True)

        @block.vector
        def _(dve):
            def x_stats(b, t):
                if t == 0:
                    dve.wait_ge(x_in, 16 * (b + 1))
                dve.bn_stats(xst[:, t, :], x_sb[:, t, :]).then_inc(xstat, 1)
                dve.wait_ge(xstat, TT * b + t + 1)
                dve.nop(nofuse=True)
                dve.bn_aggr(xmv[:, t, :], xst[:, t, :]).then_inc(xaggr, 1)

            def x_norm(b, f):
                dve.wait_ge(x_kept, FT * b + f + 1)
                dve.wait_ge(stats_in, 16 * (b + 1))
                mean, deviation = [stats_bc[:, :, i, :].rearrange("q p t -> q t p") for i in range(2)]
                v = xhatT[:, f, :].rearrange("q (t p) -> q t p", t=TT)
                dve.tensor_tensor(v, v, mean, ALU.subtract).then_inc(centred, 1)
                dve.wait_ge(centred, FT * b + f + 1)
                dve.tensor_tensor(v, v, deviation, ALU.mult).then_inc(xhat_done, 1)

            def y_mul(b, t):
                dve.wait_ge(rows_in[t], 16 * (b + 1))
                dve.wait_ge(xrs_done, b + 1)
                wait(dve, tr_ready, TRS * b)
                if isinstance(b, int) and b == 0 and t == 0:
                    dve.wait_ge(tables_ready, 2)
                dve.scalar_tensor_tensor(y_sb[:, t, :], x_sb[:, t, :], xmv[:, t, 0:1], pw_rows[:, t, 0:D],
                                         ALU.subtract, ALU.mult).then_inc(ymul, 1)

            def y_add(b, t):
                n = TT * b + t + 1
                dve.wait_ge(ymul, n)
                dve.scalar_tensor_tensor(y_sb[:, t, :], y_sb[:, t, :], xrs[:, t:t + 1], pw_rows[:, t, D:2 * D],
                                         ALU.mult, ALU.add).then_inc(yadd, 1)
                dve.wait_ge(yadd, n)
                dve.bn_stats(yst[:, t, :], y_sb[:, t, :]).then_inc(ystat, 1)
                dve.wait_ge(ystat, n)
                dve.nop(nofuse=True)
                dve.bn_aggr(ymv[:, t, :], yst[:, t, :]).then_inc(yaggr, 1)

            def y_norm(b, t):
                n = TT * b + t + 1
                dve.wait_ge(yaggr, n)
                dve.wait_ge(class_rows_in[t], 16 * (b + 1))
                dve.scalar_tensor_tensor(y_sb[:, t, :], y_sb[:, t, :], ymv[:, t, 0:1], pw_rows[:, t, 0:D],
                                         ALU.subtract, ALU.mult).then_inc(yscaled, 1)
                dve.wait_ge(yscaled, n)
                dve.wait_ge(yrs_done, n)
                dve.tensor_scalar(y_sb[:, t, :], y_sb[:, t, :], yrs[:, t:t + 1], None, ALU.mult).then_inc(yhat_done, 1)

            def compare(b):
                dve.wait_ge(ids_in, 32 * (b + 1))
                wait(dve, picked, PICKS * b)
                if isinstance(b, int) and b == 1:
                    dve.wait_ge(first_done, FT * (CLASS_AT + 1))
                dve.tensor_scalar(onehot[:, :], ids_sb[:, :], cls_val[:, 0:1], None, ALU.is_equal).then_inc(onehot_ready, 1)

            def make(b, kk):
                kind, f = ORDER[kk]
                if kind == "h":
                    return
                if kind == "x":
                    dve.wait_ge(x_hi_done, FT * b + f + 1)
                    dve.wait_ge(x_kept, FT * b + f + 1)
                    dve.tensor_tensor(cat_lo[:, kk % RING, :], xhatT[:, f, :], cat_hi[:, kk % RING, :].bitcast(f32),
                                      ALU.subtract).then_inc(x_lo_done, 1)
                    return
                n = MODS * b + MOD_BEFORE[kk]
                dve.wait_ge(xhat_done, FT * b + f + 1)
                dve.wait_ge(picked, PICKS * b + PICK_BEFORE[kk] + 1)
                wait(dve, m_lo_done, n - 1)
                dve.tensor_tensor(v_sb[:, MOD_BEFORE[kk] % 2, :], made_ps[:, kk % 2, :], xhatT[:, f, :],
                                  ALU.mult).then_inc(v_done, 1)

            def out_buffer(t, tail):
                return xhatT[:, t, :] if tail else o_sb[:, :]

            def out_stats(b, t, tail=False):
                n = TT * b + t + 1
                dve.wait_ge(second_done, n + TT)
                o = out_buffer(t, tail)
                if not tail:
                    wait(dve, out_ready, n - 1)
                dve.tensor_tensor(o, o_ps[:, t % 2, :], b2_bc, ALU.add).then_inc(o_done, 1)
                dve.wait_ge(o_done, n + 1)
                dve.bn_stats(fst[:, t, :], o).then_inc(fstat, 1)
                dve.wait_ge(fstat, n)
                dve.nop(nofuse=True)
                dve.bn_aggr(fmv[:, t, :], fst[:, t, :]).then_inc(faggr, 1)
                dve.wait_ge(faggr, n)
                dve.scalar_tensor_tensor(o, o, fmv[:, t, 0:1], g_bc,
                                         ALU.subtract, ALU.mult).then_inc(fnum, 1)

            def out_sum(b, t, par, tail=False):
                o = out_buffer(t, tail)
                n = TT * b + t + 1
                dve.wait_ge(fnum, n)
                dve.wait_ge(frs_done, n)
                dve.wait_ge(xbe_done, n)
                dve.scalar_tensor_tensor(xbe[:, par, t, :], o, frs[:, t:t + 1], xbe[:, par, t, :],
                                         ALU.mult, ALU.add).then_inc(out_ready, 1)

            def hidden_parts(b, h):
                dve.wait_ge(z_done, FT * b + h + 1)
                dve.wait_ge(second_done, TT * (b + 1))
                dve.tensor_copy(hid_hi[:, h, :], z_sb[:, h, :]).then_inc(hid_hi_done, 1)
                dve.wait_ge(hid_hi_done, FT * b + h + 1)
                dve.tensor_tensor(hid_lo[:, h, :], z_sb[:, h, :], hid_hi[:, h, :].bitcast(f32),
                                  ALU.subtract).then_inc(last_lo_done, 1)

            def link(ins):
                links[0] += 1
                ins.then_inc(dve_chain, 1)
                dve.wait_ge(dve_chain, links[0])

            def sum_blocks(i):
                v = z_sb[:, i % 2, :]
                dve.wait_ge(act_began, i + 1)
                for j in (1, 2):
                    n = NETS * i + j
                    stage_wait(dve, n)
                    dve.scalar_tensor_tensor(v, stage[n % STAGE], w_mix[:, 2 + j:3 + j], v,
                                             ALU.mult, ALU.add).then_inc(dve_used, 1)
                    dve.wait_ge(dve_used, (NETS - 1) * i + j)

            def prepare(i, dst_hi, dst_lo):
                v = z_sb[:, i % 2, :]
                dve.wait_ge(w_hi_done, i + 1)
                dve.tensor_tensor(dst_lo, v, dst_hi.bitcast(f32), ALU.subtract).then_inc(w_lo_done, 1)

            def prepare_w1(i):
                prepare(i, w1_hi[:, i, :], w1_lo[:, i, :])

            def prepare_w2(k):
                prepare(KT + k, w2_hi[:, k, :], w2_lo[:, k, :])

            def class_rows():
                dve.wait_ge(pe_used, used(PE_TILES, MOD[-1]))
                link(dve.tensor_copy(class_bias[:, :], o_ps[:, 1, :]))
                for base in (CLS_LO, SCL_LO):
                    rows = slice(base, base + 32)
                    dve.tensor_tensor(class_bias[rows, :], o_ps[rows, 1, :], class_bias[rows, :].bitcast(f32),
                                      ALU.subtract).then_inc(class_bias_ready, 1)

            def nets_stats():
                dve.wait_ge(pe_used, used(PE_TILES, NETW2 + NETS * FT - 1))
                dve.wait_ge(net_rows_in, 16)
                link(dve.tensor_tensor(net_h[:, :], o_ps[0:NB, 0, :], net_rows[:, 0, :], ALU.add))
                link(dve.bn_stats(nst[0:NB, :], net_h[:, :]))
                dve.bn_aggr(nmv[0:NB, :], nst[0:NB, :]).then_inc(net_stats, 1)

            def nets_norm():
                dve.wait_ge(net_rs, 1)
                link(dve.tensor_scalar(net_h[:, :], net_h[:, :], nmv[0:NB, 0:1], nrs[0:NB, 1:2],
                                       ALU.subtract, ALU.mult))
                link(dve.tensor_tensor(net_h[:, :], net_h[:, :], net_rows[:, 1, :], ALU.mult))
                dve.tensor_tensor(net_h[:, :], net_h[:, :], net_rows[:, 2, :], ALU.add).then_inc(m_rows, 1)

            def nets_weigh():
                dve.wait_ge(net_turned, 1)
                turned = o_ps[:, 0, 0:FT * NB].rearrange("p (k q) -> p k q", q=NB)
                for n in range(NETS):
                    cols = slice(BATCHES * n, BATCHES * (n + 1))
                    dve.tensor_scalar(mT[:, :, cols], turned[:, :, cols], w_mix[:, 2 + n:3 + n], None,
                                      ALU.mult).then_inc(mT_ready, 1)

            def batch_copy():
                dve.wait_ge(pe_used, len(PE_TILES))
                dve.tensor_copy(net_h[0:BATCHES, :], o_ps[0:BATCHES, 1, :]).then_inc(batch_rows, 1)

            def add_b1():
                dve.wait_ge(batch_turned, 1)
                for h in range(FT):
                    dve.tensor_scalar(batch_bias[:, h, :], o_ps[:, 0, h * BATCHES:(h + 1) * BATCHES],
                                      ib1_cols[:, h:h + 1], None, ALU.add).then_inc(batch_bias_ready, 1)

            links = [0]
            dve.wait_ge(small_in, 16)
            link(dve.reduce_max(w_tmp[:, 1:2], w_mix, AX.X))
            dve.tensor_scalar(w_tmp[:, 0:1], w_tmp[:, 1:2], -1.0, None, ALU.mult).then_inc(mix_max, 1)
            dve.wait_ge(mix_exp, 1)
            link(dve.reduce_sum(w_tmp[:, 2:3], w_mix, AX.X))
            link(dve.reciprocal(w_tmp[:, 3:4], w_tmp[:, 2:3]))
            dve.tensor_scalar(w_mix, w_mix, w_tmp[:, 3:4], None, ALU.mult).then_inc(mix_ready, 1)
            dve.wait_ge(mix_ready, 1)
            dve.wait_ge(cols_cleared, 1)
            for i, (kind, f) in enumerate(ORDER[FT:]):
                n_cls, bases = CLASS_OF[kind]
                for base in bases:
                    dve.tensor_scalar(class_cols[:, i, base:base + n_cls], shifts[:, FT * "tsh".index(kind) + f, 0:n_cls],
                                      w_mix[:, SOURCE[kind]:SOURCE[kind] + 1], None, ALU.mult).then_inc(shifts_ready, 1)
            for kk in range(FT):
                sum_blocks(kk)
                make(0, kk)
                if kk == 1:
                    for t in range(TT):
                        x_stats(0, t)
            dve.memset(w_tmp[:, 0:1], 0.0).then_inc(o_done, 1)
            compare(0)
            for kk in range(FT, FT + AHEAD):
                if ORDER[kk][0] == "t":
                    x_norm(0, ORDER[kk][1])
                make(0, kk)
                prepare_w1(kk)

            def chunk(b, par, first=False, last=False):
                for k in range(KT):
                    kk = k + AHEAD
                    if first:
                        if kk < FT + AHEAD:
                            continue
                        for j in PREP_AT.get(k, ()):
                            prepare_w1(j)
                        for j in PREP2_AT.get(k, ()):
                            prepare_w2(j)
                        if k == CLASS_AT - 1:
                            class_rows()
                        if k == NORM_AT - 1:
                            nets_stats()
                        if k == NORM_AT:
                            nets_norm()
                        if k == TURN_AT + 1:
                            nets_weigh()
                        if k == KT - 1:
                            batch_copy()
                    if kk < KT:
                        make(b, kk)
                    elif not last:
                        make(b + 1, kk - KT)
                    if k in X_NORM_AT[first]:
                        x_norm(b, X_NORM_AT[first].index(k) + (FT - len(X_NORM_AT[first])))
                    for t in range(TT):
                        if Y_NORM_AT[first][t] == k:
                            y_norm(b, t)
                    for t in range(TT):
                        if Y_MUL_AT[first][t] == k:
                            y_mul(b, t)
                    if k in Y_STATS_AT[first]:
                        y_add(b, Y_STATS_AT[first].index(k))
                    if not first and k in OUT_AT:
                        out_stats(b - 1, OUT_AT.index(k))
                    if not first and k in SUM_AT:
                        out_sum(b - 1, SUM_AT.index(k), 1 - par)
                    if not last:
                        if k in GATHER_AT:
                            x_stats(b + 1, GATHER_AT.index(k))
                        if k == 13:
                            compare(b + 1)
                if first:
                    add_b1()

            chunk(0, 0, first=True)
            with dve.Fori(0, BATCHES // 2 - 1) as pair:
                b = 2 * pair + 1
                chunk(b, 1)
                chunk(b + 1, 0)
            chunk(BATCHES - 1, 1, last=True)
            for h in range(FT):
                hidden_parts(BATCHES - 1, h)
            for t in range(TT):
                out_stats(BATCHES - 1, t, tail=True)
                if t > 0:
                    out_sum(BATCHES - 1, t - 1, 1, tail=True)
            out_sum(BATCHES - 1, TT - 1, 1, tail=True)

        @block.tensor
        def _(pe):
            def class_sum(i):
                pe.wait_ge(shifts_ready, 2 * MODS)
                stage_wait(pe, MOD[i])
                pe.matmul(o_ps[:, 1, :], class_cols[:, i, :], stage[MOD[i] % STAGE], start=(i == 0),
                          stop=(i == MODS - 1)).then_inc(pe_used, 1)

            def nets_hidden(n):
                parts = (0, 1) if n == 0 else (n + 1,)
                for c in parts:
                    stage_wait(pe, NET[c])
                for h in range(FT):
                    i = n * FT + h
                    for c in parts:
                        depth = tiles[NET[c]][1]
                        ins = pe.matmul(o_ps[:, 0, i * BATCHES:(i + 1) * BATCHES],
                                        stage[NET[c] % STAGE][0:depth, h * P:(h + 1) * P], sT[0:depth, c, :],
                                        start=(c == parts[0]), stop=(c == parts[-1]))
                ins.then_inc(pe_used, len(parts))

            def nets_output(i):
                if i == 0:
                    pe.wait_ge(net_silu, NETS * FT)
                stage_wait(pe, NETW2 + i)
                pe.matmul(o_ps[0:NB, 0, :], net_hidT[:, i, :], stage[(NETW2 + i) % STAGE], start=(i == 0),
                          stop=(i == NETS * FT - 1)).then_inc(pe_used, 1)

            def nets_turn():
                pe.wait_ge(m_rows, 1)
                for k in range(FT):
                    ins = pe.transpose(o_ps[:, 0, k * NB:(k + 1) * NB], net_h[:, k * P:(k + 1) * P], ident[0:NB, 0:NB])
                ins.then_inc(net_turned, 1)

            def batch_sum(i):
                if i == 0:
                    pe.wait_ge(mT_ready, NETS)
                    pe.wait_ge(class_bias_ready, 2)
                k, j = i // NETS, i % NETS
                stage_wait(pe, BIAS0 + i)
                pe.matmul(o_ps[0:BATCHES, 1, :], mT[:, k, BATCHES * j:BATCHES * (j + 1)],
                          stage[(BIAS0 + i) % STAGE], start=(i == 0),
                          stop=(i == NETS * FT - 1)).then_inc(pe_used, 1)

            def batch_turn():
                pe.wait_ge(batch_rows, 1)
                for k in range(FT):
                    ins = pe.transpose(o_ps[:, 0, k * BATCHES:(k + 1) * BATCHES],
                                       net_h[0:BATCHES, k * P:(k + 1) * P], ident[0:BATCHES, 0:BATCHES])
                ins.then_inc(batch_turned, 1)

            def make(b, kk):
                kind, f = ORDER[kk]
                before = kk - 2
                kind_before, f_before = ORDER[before]
                done, per, nth = {"x": (x_kept, FT, f_before), "h": (t_copied, FT, f_before)}.get(
                    kind_before, (v_done, PICKS, PICK_BEFORE[before]))
                wait(pe, done, per * (b if before >= 0 else b - 1) + nth + 1)
                if kind in "xh":
                    if kind == "x":
                        pe.wait_ge(x_in, 16 * (b + 1))
                    if kind == "h" and f == 0:
                        pe.wait_ge(yhat_done, TT * (b + 1))
                    src = x_sb if kind == "x" else y_sb
                    for t in range(TT):
                        ins = pe.transpose(made_ps[:, kk % 2, t * P:(t + 1) * P], src[:, t, f * P:(f + 1) * P], ident)
                    ins.then_inc(tr_ready, 1)
                if kind in "ts":
                    pe.wait_ge(onehot_ready, b + 1)
                    if isinstance(b, int):
                        pe.wait_ge(tables_ready, 2)
                    pe.matmul(made_ps[:, kk % 2, :], class_tab[:, "ts".index(kind), f * P:(f + 1) * P], onehot[:, :],
                              start=True, stop=True).then_inc(picked, 1)

            def first_ready(b, k, bias_last=False):
                if bias_last and k < FT:
                    pe.wait_ge(sum_lo_done, k + 1)
                elif bias_last:
                    pe.wait_ge(w_lo_done, k + 1 - FT)
                if k < FT:
                    pe.wait_ge(x_lo_done, FT * b + k + 1)
                else:
                    pe.wait_ge(m_lo_done, MODS * b + MOD_BEFORE[k] + 1)

            def first_part(k, h, start):
                hi, lo = cat_hi[:, k % RING, :], cat_lo[:, k % RING, :]
                cols = slice(h * P, (h + 1) * P)
                acc = hid_ps[:, h, :]
                pe.matmul(acc, w1_hi[:, k, cols], hi, start=start, stop=False)
                pe.matmul(acc, w1_hi[:, k, cols], lo, start=False, stop=False)
                pe.matmul(acc, w1_lo[:, k, cols], hi, start=False, stop=(k == KT - 1)).then_inc(first_done, 1)

            def first(b, k, bias_last=False):
                first_ready(b, k, bias_last)
                for h in range(FT):
                    if k == 0:
                        wait(pe, z_done, FT * (b - 1) + h + 1)
                    if k == (CLASS_AT if bias_last else 0):
                        pe.wait_ge(onehot_ready, b + 1)
                        pe.wait_ge(class_bias_ready, 2)
                        pe.matmul(hid_ps[:, h, :], class_bias[:, h * P:(h + 1) * P], onehot[:, :],
                                  start=(k == 0), stop=False)
                    first_part(k, h, start=(bias_last and k == 0))
                    if bias_last and k == KT - 1 and h == 1:
                        batch_turn()

            def second(b, t):
                pe.wait_ge(hid_lo_done, FT * (b + 2))
                pe.wait_ge(o_done, TT * b + t)
                for k in range(FT):
                    ins = second_part(o_ps[:, t % 2, :], t, k)
                ins.then_inc(second_done, 1)

            def second_part(acc, t, k):
                cols = slice(t * P, (t + 1) * P)
                pe.matmul(acc, hid_hi[:, k, cols], w2_hi[:, k, :], start=(k == 0), stop=False)
                pe.matmul(acc, hid_lo[:, k, cols], w2_hi[:, k, :], start=False, stop=False)
                return pe.matmul(acc, hid_hi[:, k, cols], w2_lo[:, k, :], start=False, stop=(k == FT - 1))

            def last_tiles(b):
                for k in range(KT - RING, KT - 1):
                    first_ready(b, k)
                    for h in (0, 1):
                        first_part(k, h, start=False)
                first_ready(b, KT - 1)
                for h in (0, 1):
                    first_part(KT - 1, h, start=False)
                for h in (2, 3):
                    for k in range(KT - RING, KT):
                        first_part(k, h, start=False)

            pe.wait_ge(small_in, 16)
            pe.transpose(made_ps[:, 1, 0:P], ident, ident).then_inc(second_done, TT)
            for kk in range(AHEAD):
                make(0, kk)

            def chunk(b, first_chunk=False, last=False):
                for k in range(KT):
                    kk = k + AHEAD
                    if first_chunk and k < FT:
                        pass
                    elif kk < KT:
                        make(b, kk)
                    elif not last:
                        make(b + 1, kk - KT)
                    if last and k == KT - RING:
                        last_tiles(b)
                        return
                    first(b, k, bias_last=first_chunk)
                    if first_chunk:
                        if k == 0:
                            make(b, AHEAD)
                        for i in CLASS_SUM_AT.get(k, ()):
                            class_sum(i)
                        if k == FT - 1:
                            for i in range(AHEAD):
                                make(b, FT + i)
                                class_sum(2 + i)
                        if k == HIDDEN_AT:
                            for n in range(NETS):
                                nets_hidden(n)
                        for i in NET_OUTPUT_AT.get(k, ()):
                            nets_output(i)
                        if k == TURN_AT:
                            nets_turn()
                        for i in BATCH_SUM_AT.get(k, ()):
                            batch_sum(i)
                    if not first_chunk and k in SECOND_AT:
                        second(b - 1, SECOND_AT.index(k))
                if first_chunk:
                    pe.wait_ge(w_lo_done, KT)

            chunk(0, first_chunk=True)
            with pe.Fori(0, BATCHES // 2 - 1) as pair:
                b = 2 * pair + 1
                chunk(b)
                chunk(b + 1)
            chunk(BATCHES - 1, last=True)
            for t in range(TT):
                pe.wait_ge(o_done, TT * (BATCHES - 1) + t)
                for k in range(FT):
                    pe.wait_ge(last_lo_done, k + 1)
                    ins = second_part(o_ps[:, t % 2, :], t, k)
                ins.then_inc(second_done, 1)


_NETS = ["mem", "noi", "res"]


def kernel(**inputs):
    import concourse.bacc as bacc
    from concourse.bass_utils import run_bass_kernel_spmd

    nc = bacc.Bacc("TRN2", target_bir_lowering=False, num_devices=1)
    arrays = {}

    def put(name, a):
        a = np.ascontiguousarray(a)
        arrays[name] = a
        return nc.dram_tensor(name, a.shape, mybir.dt.from_np(a.dtype), kind="ExternalInput").ap()

    def given(name):
        return np.asarray(inputs[name])

    def cond(name):
        return given("L0_cond_" + name)

    def by_column(ids):
        return ids.reshape(BATCHES, P, TT).transpose(0, 2, 1).reshape(BATCHES, TOKENS)

    def cols(v):
        return v.reshape(FT, P).T

    def turned(tab):
        t = tab.T.reshape(FT, P, -1).transpose(1, 0, 2)
        return np.pad(t, ((0, 0), (0, 0), (0, 5 - t.shape[2]))).reshape(P, -1)

    def features_first(v):
        t = v.T
        t = np.pad(t, ((0, -len(t) % P), (0, 0)))
        return t.reshape(-1, P, BATCHES).transpose(1, 0, 2).reshape(P, -1)

    class_of = np.full((P, 1), -1.0, np.float32)
    for base, n in ((CLS_HI, 5), (CLS_LO, 5), (SCL_HI, 3), (SCL_LO, 3)):
        class_of[base:base + n, 0] = np.arange(n)
    pieces = dict(
        aw=np.broadcast_to(cond("aw"), (P, 6)),
        identity=np.eye(P, dtype=np.float32),
        class_of=class_of,
        b1T=np.concatenate([cols(cond(n + "_b1")) for n in _NETS], axis=1),
        ib1T=cols(cond("int_b1")),
        sT=np.concatenate([features_first(given(n)) for n in ("cond_512", "cond_64", "fside_Bx32_0")], axis=1),
        shifts=np.concatenate([turned(cond(n)) for n in ("tm_b", "ms_b", "cp_b")], axis=1),
    )
    small_at, at = {}, 0
    for name, piece in pieces.items():
        small_at[name] = (at, piece.shape[1])
        at += piece.shape[1]
    scales = np.zeros((P, 2, D), np.float32)
    for i, (name, bases) in enumerate((("tm_g", (CLS_HI, CLS_LO)), ("ms_g", (SCL_HI, SCL_LO)))):
        for base in bases:
            scales[base:base + len(cond(name)), i] = cond(name)
    net_vecs = np.stack([np.stack([cond(n + v) for v in ("_b2", "_g", "_be")]) for n in _NETS])
    cls, scl = given("itok_BxS_0_4"), given("mask_BxS_ik0")
    pathway = given("itok_BxS_0_999")
    args = dict(
        x=put("x", given("x")),
        ids=put("ids", np.stack([by_column(cls), by_column(scl)])),
        pid=put("pid", np.stack([pathway.reshape(BATCHES, P, TT), cls.reshape(BATCHES, P, TT)], axis=2)
                .transpose(1, 0, 2, 3).reshape(P, BATCHES * 2 * TT)),
        cp=put("cp", cond("cp_g")),
        small=put("small", np.concatenate(list(pieces.values()), axis=1)), small_at=small_at,
        scales=put("scales", scales),
        rows=put("rows", np.stack([cond("int_b2"), cond("int_g"), cond("int_be")])),
        net_vecs=put("net_vecs", np.repeat(net_vecs, BATCHES, axis=0)),
        pw=put("pw", np.concatenate([cond("pw_g"), cond("pw_b")], axis=1)),
        W1s=[put(n + "_W1", cond(n + "_W1")) for n in _NETS],
        W2s=[put(n + "_W2", cond(n + "_W2")) for n in _NETS],
        int_W1=put("int_W1", cond("int_W1")), int_W2=put("int_W2", cond("int_W2")),
        out=nc.dram_tensor("out", (BATCHES, TOKENS, D), mybir.dt.float32, kind="ExternalOutput").ap(),
    )
    build(nc, **args)
    r = run_bass_kernel_spmd(nc, [arrays], core_ids=[0])
    return r.results[0]["out"]
```
